# Optimizing a Trainium2 kernel written in Bass

```python
import numpy as np
import jax
import jax.numpy as jnp

def _softmax(x, axis=-1):
    return jax.nn.softmax(x, axis=axis)

def _gelu(x):
    return jax.nn.gelu(x, approximate=True)

def _silu(x):
    return jax.nn.silu(x)

def _sigmoid(x):
    return jax.nn.sigmoid(x)

def _layernorm(x, axis=-1, eps=1e-05):
    m = jnp.mean(x, axis=axis, keepdims=True)
    v = jnp.var(x, axis=axis, keepdims=True)
    return (x - m) / jnp.sqrt(v + eps)

def _scatter_add(tgt, idx, src, axis=0):
    return tgt.at[idx].add(src)

def _segment_sum(src, seg, n):
    return jax.ops.segment_sum(src, seg, n)
kernel_name = 'mk_perceiver_d1_seqx_r2_2ac3cc'

def setup_inputs(seed: int=0):
    np.random.seed(seed)
    _w = jnp.asarray

    def _rec_inputs():
        import jax
        import jax.numpy as jnp
        _rk = jax.random.key(seed)
        x = 7.22e-05 + 1 * jax.random.normal(jax.random.fold_in(_rk, 1), (8, 64, 512), jnp.float32)
        _lenS = 64 - jax.random.randint(jax.random.fold_in(_rk, 7), (8,), 0, max(1, 64 // 4) + 1, jnp.int32)
        _lenS2 = 512 - jax.random.randint(jax.random.fold_in(_rk, 8), (8,), 0, max(1, 512 // 4) + 1, jnp.int32)
        _ctx_1024P = jax.random.normal(jax.random.fold_in(_rk, 11), (8, 16, 512), jnp.float32)
        _ctx_1024c = jax.random.dirichlet(jax.random.fold_in(_rk, 511), 0.3 * jnp.ones((16,), jnp.float32), (8, 512))
        _ctx_1024t = jnp.einsum('bsk,bkd->bsd', _ctx_1024c, _ctx_1024P)
        _ctx_1024t = _ctx_1024t * jax.lax.rsqrt(jnp.mean(jnp.square(_ctx_1024t)) + 1e-12) * 0.953939
        ctx_1024 = 4.13588e-05 + 0.999923 * (_ctx_1024t + 0.3 * jax.random.normal(jax.random.fold_in(_rk, 611), (8, 512, 512), jnp.float32))
        return (x, ctx_1024)
    x, ctx_1024 = _rec_inputs()

    def _L0_xattn_setup():
        import jax, jax.numpy as jnp
        import numpy as np
        B, S, D, H = (4, 1024, 512, 16)
        HD = D // H
        key = jax.random.key(seed)
        ks = jax.random.split(key, 11)
        s = 1.0 / np.sqrt(D)
        return {'q': jax.random.normal(ks[0], (B, S, D), jnp.float32), 'k': jax.random.normal(ks[1], (B, S, D), jnp.float32), 'v': jax.random.normal(ks[2], (B, S, D), jnp.float32), 'Wq': jax.random.normal(ks[3], (D, D), jnp.float32) * s, 'bq': jnp.zeros((D,), jnp.float32), 'Wk': jax.random.normal(ks[4], (D, D), jnp.float32) * s, 'bk': jnp.zeros((D,), jnp.float32), 'Wv': jax.random.normal(ks[5], (D, D), jnp.float32) * s, 'bv': jnp.zeros((D,), jnp.float32), 'Wo': jax.random.normal(ks[6], (D, D), jnp.float32) * s, 'bo': jnp.zeros((D,), jnp.float32)}
    _L0_xattn_all = _L0_xattn_setup()
    _L0_xattn_in = {k: v for k, v in _L0_xattn_all.items() if k in ('Wq', 'bq', 'Wk', 'bk', 'Wv', 'bv', 'Wo', 'bo')}
    del _L0_xattn_all

    def _L0_attn_setup():
        import jax, jax.numpy as jnp
        import numpy as np
        DIM = 512
        HEADS = 16
        HEAD_DIM = DIM // HEADS
        FEAT = 128
        B, N = (4, 2048)

        def _elu1(x):
            return jnp.where(x > 0, x + 1.0, jnp.exp(x))
        key = jax.random.key(seed)
        k_x, k_qkv, k_proj, k_wo, k_bo = jax.random.split(key, 5)
        x = jax.random.normal(k_x, (B, N, DIM), dtype=jnp.float32)
        w_qkv = jax.random.normal(k_qkv, (DIM, 3 * DIM), dtype=jnp.float32) * (1.0 / np.sqrt(DIM))
        proj_matrix = jax.random.normal(k_proj, (HEADS, HEAD_DIM, FEAT), dtype=jnp.float32) * (1.0 / np.sqrt(HEAD_DIM))
        w_out = jax.random.normal(k_wo, (DIM, DIM), dtype=jnp.float32) * (1.0 / np.sqrt(DIM))
        b_out = jax.random.normal(k_bo, (DIM,), dtype=jnp.float32) * 0.01
        return {'x': x, 'w_qkv': w_qkv, 'proj_matrix': proj_matrix, 'w_out': w_out, 'b_out': b_out}
    _L0_attn_all = _L0_attn_setup()
    _L0_attn_in = {k: v for k, v in _L0_attn_all.items() if k in ('w_qkv', 'proj_matrix', 'w_out', 'b_out')}
    del _L0_attn_all

    def _L0_ffn_setup():
        import jax, jax.numpy as jnp
        import numpy as np
        B, S, D = (4, 2048, 512)
        E, F_EXP = (16, 1024)
        F_C = 2.0
        F_SH = 1024
        key = jax.random.key(seed)
        ks = jax.random.split(key, 8)
        s = 0.02
        return {'hidden_states': jax.random.normal(ks[0], (B, S, D), jnp.float32), 'gate_w': jax.random.normal(ks[1], (E, D), jnp.float32) * s, 'Wg': jax.random.normal(ks[2], (E, F_EXP, D), jnp.float32) * s, 'Wu': jax.random.normal(ks[3], (E, F_EXP, D), jnp.float32) * s, 'Wd': jax.random.normal(ks[4], (E, D, F_EXP), jnp.float32) * s, 'Ws_g': jax.random.normal(ks[5], (F_SH, D), jnp.float32) * s, 'Ws_u': jax.random.normal(ks[6], (F_SH, D), jnp.float32) * s, 'Ws_d': jax.random.normal(ks[7], (D, F_SH), jnp.float32) * s}
    _L0_ffn_all = _L0_ffn_setup()
    _L0_ffn_in = {k: v for k, v in _L0_ffn_all.items() if k in ('gate_w', 'Wg', 'Wu', 'Wd', 'Ws_g', 'Ws_u', 'Ws_d')}
    del _L0_ffn_all
    return {'x': x, 'ctx_1024': ctx_1024, 'L0_xattn_Wq': _L0_xattn_in['Wq'], 'L0_xattn_bq': _L0_xattn_in['bq'], 'L0_xattn_Wk': _L0_xattn_in['Wk'], 'L0_xattn_bk': _L0_xattn_in['bk'], 'L0_xattn_Wv': _L0_xattn_in['Wv'], 'L0_xattn_bv': _L0_xattn_in['bv'], 'L0_xattn_Wo': _L0_xattn_in['Wo'], 'L0_xattn_bo': _L0_xattn_in['bo'], 'L0_attn_w_qkv': _L0_attn_in['w_qkv'], 'L0_attn_proj_matrix': _L0_attn_in['proj_matrix'], 'L0_attn_w_out': _L0_attn_in['w_out'], 'L0_attn_b_out': _L0_attn_in['b_out'], 'L0_ffn_gate_w': _L0_ffn_in['gate_w'], 'L0_ffn_Wg': _L0_ffn_in['Wg'], 'L0_ffn_Wu': _L0_ffn_in['Wu'], 'L0_ffn_Wd': _L0_ffn_in['Wd'], 'L0_ffn_Ws_g': _L0_ffn_in['Ws_g'], 'L0_ffn_Ws_u': _L0_ffn_in['Ws_u'], 'L0_ffn_Ws_d': _L0_ffn_in['Ws_d']}

def reference(x, ctx_1024, L0_xattn_Wq, L0_xattn_bq, L0_xattn_Wk, L0_xattn_bk, L0_xattn_Wv, L0_xattn_bv, L0_xattn_Wo, L0_xattn_bo, L0_attn_w_qkv, L0_attn_proj_matrix, L0_attn_w_out, L0_attn_b_out, L0_ffn_gate_w, L0_ffn_Wg, L0_ffn_Wu, L0_ffn_Wd, L0_ffn_Ws_g, L0_ffn_Ws_u, L0_ffn_Ws_d):
    import jax
    import jax.numpy as jnp

    def _L0_xattn_ref(q, k, v, Wq, bq, Wk, bk, Wv, bv, Wo, bo):
        import jax, jax.numpy as jnp
        import numpy as np
        B, S, D, H = (4, 1024, 512, 16)
        HD = D // H
        b, n, _ = q.shape
        qh = (q @ Wq + bq).reshape(b, n, H, HD)
        kh = (k @ Wk + bk).reshape(b, k.shape[1], H, HD)
        vh = (v @ Wv + bv).reshape(b, v.shape[1], H, HD)
        scale = 1.0 / np.sqrt(HD)
        scores = jnp.einsum('blhe,bshe->bhls', qh, kh)
        attn = jax.nn.softmax(scale * scores, axis=-1)
        out = jnp.einsum('bhls,bshd->blhd', attn, vh)
        out = out.reshape(b, n, H * HD)
        return out @ Wo + bo

    def _L0_attn_ref(x, w_qkv, proj_matrix, w_out, b_out):
        import jax, jax.numpy as jnp
        import numpy as np
        DIM = 512
        HEADS = 16
        HEAD_DIM = DIM // HEADS
        FEAT = 128
        B, N = (4, 2048)

        def _elu1(x):
            return jnp.where(x > 0, x + 1.0, jnp.exp(x))
        b, n, d = x.shape
        h, hd = (HEADS, HEAD_DIM)
        qkv = x @ w_qkv
        q, k, v = jnp.split(qkv, 3, axis=-1)
        to_heads = lambda t: t.reshape(b, n, h, hd).transpose(0, 2, 1, 3)
        q, k, v = (to_heads(q), to_heads(k), to_heads(v))
        q_proj = _elu1(jnp.einsum('bhnd,hdf->bhnf', q, proj_matrix))
        k_proj = _elu1(jnp.einsum('bhnd,hdf->bhnf', k, proj_matrix))
        kv = jnp.einsum('bhnf,bhnd->bhfd', k_proj, v)
        attn = jnp.einsum('bhnf,bhfd->bhnd', q_proj, kv)
        k_sum = k_proj.sum(axis=2)
        z = 1.0 / (jnp.einsum('bhnf,bhf->bhn', q_proj, k_sum) + 1e-08)
        attn = attn * z[..., None]
        out = attn.transpose(0, 2, 1, 3).reshape(b, n, d)
        return out @ w_out + b_out

    def _L0_ffn_ref(hidden_states, gate_w, Wg, Wu, Wd, Ws_g, Ws_u, Ws_d):
        import jax, jax.numpy as jnp
        import numpy as np
        B, S, D = (4, 2048, 512)
        E, F_EXP = (16, 1024)
        F_C = 2.0
        F_SH = 1024
        b, s, d = hidden_states.shape
        e = gate_w.shape[0]
        cap = int(s * F_C / e)
        logits = jnp.einsum('bsd,ed->bse', hidden_states, gate_w)
        scores = jax.nn.softmax(logits, axis=-1).transpose(0, 2, 1)
        topk_w, topk_idx = jax.lax.top_k(scores, cap)
        x_tok = jnp.take_along_axis(hidden_states[:, None, :, :], topk_idx[..., None], axis=2)
        g = jnp.einsum('becd,efd->becf', x_tok, Wg)
        u = jnp.einsum('becd,efd->becf', x_tok, Wu)
        h = jax.nn.gelu(g, approximate=False) * u
        eo = jnp.einsum('becf,edf->becd', h, Wd) * topk_w[..., None]
        offs = (jnp.arange(b) * s)[:, None, None]
        flat_idx = (topk_idx + offs).reshape(-1)
        flat = jnp.zeros((b * s, d), hidden_states.dtype)
        flat = flat.at[flat_idx].add(eo.reshape(-1, d))
        out = flat.reshape(b, s, d)
        gs = jnp.einsum('bsd,fd->bsf', hidden_states, Ws_g)
        us = jnp.einsum('bsd,fd->bsf', hidden_states, Ws_u)
        shared = jnp.einsum('bsf,df->bsd', jax.nn.gelu(gs, approximate=False) * us, Ws_d)
        return out + shared
    x = x + _L0_xattn_ref(_layernorm(x, axis=-1), ctx_1024, ctx_1024, L0_xattn_Wq, L0_xattn_bq, L0_xattn_Wk, L0_xattn_bk, L0_xattn_Wv, L0_xattn_bv, L0_xattn_Wo, L0_xattn_bo)
    x = x + _L0_attn_ref(_layernorm(x, axis=-1), L0_attn_w_qkv, L0_attn_proj_matrix, L0_attn_w_out, L0_attn_b_out)
    x = x + _L0_ffn_ref(_layernorm(x, axis=-1), L0_ffn_gate_w, L0_ffn_Wg, L0_ffn_Wu, L0_ffn_Wd, L0_ffn_Ws_g, L0_ffn_Ws_u, L0_ffn_Ws_d)
    return x

_drawn_inputs = setup_inputs


def setup_inputs(seed=0):
    import zlib

    import numpy as np

    out = dict(_drawn_inputs(seed))
    spreads = {'L0_xattn_bq': (0.0, 0.374),
     'L0_xattn_bk': (0.0, 2.0),
     'L0_xattn_bv': (0.0, 0.1),
     'L0_xattn_bo': (0.0, 0.1)}
    factors = {'L0_attn_proj_matrix': 8.0,
     'L0_attn_b_out': 7.081,
     'L0_ffn_gate_w': 4.957,
     'L0_ffn_Wg': 4.212,
     'L0_ffn_Wu': 4.054,
     'L0_ffn_Wd': 4.096,
     'L0_ffn_Ws_g': 2.765,
     'L0_ffn_Ws_u': 2.709}
    for name, (base, spread) in spreads.items():
        noise = np.random.default_rng([zlib.crc32(name.encode()), seed]).standard_normal(out[name].shape)
        drawn = base * np.exp(spread * noise) if base else spread * noise
        out[name] = jnp.asarray(drawn.astype(out[name].dtype))
    for name, factor in factors.items():
        out[name] = (out[name] * factor).astype(out[name].dtype)
    return out
```

```python
from contextlib import ExitStack

import numpy as np

import concourse.bass as bass
from concourse import mybir

F32 = mybir.dt.float32
F32R = mybir.dt.float32r
U32 = mybir.dt.uint32
ALU = mybir.AluOpType
ACT = mybir.ActivationFunctionType
AX = mybir.AxisListType

P = 128
B, L, S, D = 8, 64, 512, 512
H, HD, FEAT = 16, 32, 128
E, CAP, FF = 16, 8, 1024
TOK = B * L
NT = TOK // P
KT = D // P
NS = S // P
NF = FF // P
HPT = P // HD
PAIRS = H // 2
SLOTS = B * CAP
KVW = 48
LGW = 96
EPS = 1e-5
BANK = 512


def perceiver_block(nc, x_d, ctx_d, wq_d, bq_d, wk_d, bk_d, wv_d, bv_d, wo_d, bo_d, wqkv_d, proj_d,
                    wout_d, bout_d, gate_d, wg_d, wu_d, wd_d, wsg_d, wsu_d, wsd_d, out_d):
    main = ExitStack()
    with main:
        def sb(stack, name, shape, dt=F32):
            return stack.enter_context(nc.sbuf_tensor(name, shape, dt))

        def sem(name):
            return main.enter_context(nc.semaphore(name))

        x = sb(main, "x", [P, NT, D])
        xn_T = sb(main, "xn_T", [P, KT, TOK])
        ident = sb(main, "ident", [P, P])
        iota_p = sb(main, "iota_p", [P, 1])
        ones = sb(main, "ones", [P, P])
        bias_q = sb(main, "bias_q", [P, KT])
        bias_k = sb(main, "bias_k", [P, KT])
        bias_v = sb(main, "bias_v", [P, KT])
        stats = sb(main, "stats", [P, NT, 6])
        mean_var = sb(main, "mean_var", [P, NT, 2])
        var_eps = sb(main, "var_eps", [P, NT])
        std = sb(main, "std", [P, NT])
        rstd = sb(main, "rstd", [P, NT])
        newton = sb(main, "newton", [P, NT])

        early = ExitStack()
        w_qkv = sb(early, "w_qkv", [P, KT, 3 * D])
        w_o = sb(early, "w_o", [P, KT, D])
        row_bias = sb(early, "row_bias", [P, 2, D])
        cross = ExitStack()
        q_T = sb(cross, "q_T", [P, KT, TOK])
        wk_hi = sb(cross, "wk_hi", [P, KT, D], F32R)
        wk_lo = sb(cross, "wk_lo", [P, KT, D], F32R)
        wv_hi = sb(cross, "wv_hi", [P, KT, D], F32R)
        wv_lo = sb(cross, "wv_lo", [P, KT, D], F32R)
        ctx_raw = sb(cross, "ctx_raw", [P, KT, S])
        ctx_hi = sb(cross, "ctx_hi", [P, 2, KT, S], F32R)
        ctx_lo = sb(cross, "ctx_lo", [P, 2, KT, S], F32R)
        k_T = sb(cross, "k_T", [P, 2, KT, S])
        v_s = sb(cross, "v_s", [P, 2, NS, D])
        probs = sb(cross, "probs", [P, PAIRS, S])
        probs_T = sb(cross, "probs_T", [P, 2, 2, NS, P])
        q_diag = sb(cross, "q_diag", [P, KT, 2, P])
        o_T = sb(cross, "o_T", [P, KT, TOK])
        neg_max = sb(cross, "neg_max", [P, PAIRS])
        row_sum = sb(cross, "row_sum", [P, PAIRS])
        row_inv = sb(cross, "row_inv", [P, PAIRS])
        cross.close()
        xn_cross = probs
        linear = ExitStack()
        w_out = sb(linear, "w_out", [P, KT, D])
        xn_lin = sb(linear, "xn_lin", [P, NT, D])
        ql_T = sb(linear, "ql_T", [P, KT, TOK])
        kl_T = sb(linear, "kl_T", [P, KT, TOK])
        proj = sb(linear, "proj", [P, KT, HPT, FEAT])
        v_bd = sb(linear, "v_bd", [P, NT, H, 2, KVW])
        q_feat = sb(linear, "q_feat", [P, H, TOK])
        k_feat = sb(linear, "k_feat", [P, 2, NT, HPT * FEAT])
        kv = sb(linear, "kv", [P, NT, H, 2 * KVW])
        exps = sb(linear, "exps", [P, 4, BANK])
        den = sb(linear, "den", [P, 8, 8])
        den_inv = sb(linear, "den_inv", [P, 8, 8])
        linear.close()
        early.close()
        att = xn_lin
        att_T = ql_T
        moe = ExitStack()
        xn_moe = sb(moe, "xn_moe", [P, NT, D])
        w_g = sb(moe, "w_g", [P, 2, KT, FF])
        w_u = sb(moe, "w_u", [P, 2, KT, FF])
        w_d = sb(moe, "w_d", [P, 2, NF, D])
        gate = sb(moe, "gate", [P, KT, LGW])
        logit = sb(moe, "logit", [P, NT, E])
        lmax = sb(moe, "lmax", [P, NT])
        lsum = sb(moe, "lsum", [P, NT])
        linv = sb(moe, "linv", [P, NT])
        score_T = sb(moe, "score_T", [E, TOK])
        top_w = sb(moe, "top_w", [E, B, CAP])
        top_i = sb(moe, "top_i", [E, B, CAP], U32)
        top_f = sb(moe, "top_f", [E, B, CAP])
        spread_i = sb(moe, "spread_i", [P, E, SLOTS])
        spread_w = sb(moe, "spread_w", [P, E, SLOTS])
        pick = sb(moe, "pick", [P, E, SLOTS])
        pick_w = spread_i[:].rearrange("p e s -> p (e s)").rearrange("p (b e c) -> p b e c", b=B, e=E)
        x_slot = sb(moe, "x_slot", [P, KT, E, SLOTS])
        give = sb(moe, "give", [P, B, L])
        gelu = sb(moe, "gelu", [P, 2, BANK])
        hid = sb(moe, "hid", [P, 2, BANK])
        hid_T = sb(moe, "hid_T", [P, 2, KT, P])
        half = sb(moe, "half", [SLOTS, 2, D])
        eo = sb(moe, "eo", [SLOTS, 2, D])
        eo_slot = sb(moe, "eo_slot", [P, B, D])
        moe.close()

        ps = main.enter_context(nc.psum_tensor("ps", [P, 8, BANK], F32))

        def bank(n):
            return ps[:, n, :]

        x_in, wq_in, wk_in, wv_in, bias_in = (sem(f"{n}_in") for n in ("x", "wq", "wk", "wv", "bias"))
        ctx_in, wqkv_in, wo_in, wout_in, rows_in = (sem(f"{n}_in") for n in ("ctx", "wqkv", "wo", "wout", "rows"))
        proj_in, gate_in = sem("proj_in"), sem("gate_in")
        wg_in, wu_in, wd_in = ([sem(f"{n}_in{i}") for i in range(2)] for n in ("wg", "wu", "wd"))
        consts = sem("consts")
        chain = sem("dve_chain")
        stats_done, std_done, xn_done = sem("stats_done"), sem("std_done"), sem("xn_done")
        xnT_ps, xnT_act, xnT_dve = sem("xnT_ps"), sem("xnT_act"), sem("xnT_dve")
        w_hi, w_split = sem("w_hi"), sem("w_split")
        ctx_hi_done, ctx_split = sem("ctx_hi_done"), sem("ctx_split")
        k_ps, k_done, v_ps, v_done = sem("k_ps"), sem("k_done"), sem("v_ps"), sem("v_done")
        q_ps, q_done, diag_done = sem("q_ps"), sem("q_done"), sem("diag_done")
        score_ps, max_done, exp_done, inv_done, prob_done = (
            sem("score_ps"), sem("max_done"), sem("exp_done"), sem("inv_done"), sem("prob_done"))
        pT_ps = sem("pT_ps")
        pT_done = [sem("pT_done_act"), sem("pT_done_dve")]
        o_ps, o_done = sem("o_ps"), sem("o_done")
        xbias_done, res_ps, x_done = sem("xbias_done"), sem("res_ps"), sem("x_done")
        qkv_ps, qkv_act, qkv_dve = sem("qkv_ps"), sem("qkv_act"), sem("qkv_dve")
        vbd_zero = sem("vbd_zero")
        feat_ps, fexp_done, fmin_done, feat_done = (
            sem("feat_ps"), sem("fexp_done"), sem("fmin_done"), sem("feat_done"))
        kv_ps, kv_done, att_ps, att_done = sem("kv_ps"), sem("kv_done"), sem("att_ps"), sem("att_done")
        attT_ps, attT_act, attT_dve = sem("attT_ps"), sem("attT_act"), sem("attT_dve")
        logit_ps, lsub_done, lexp_done, score_done = (
            sem("logit_ps"), sem("lsub_done"), sem("lexp_done"), sem("score_done"))
        scoreT_ps, spread_done, pick_ps, pick_done = (
            sem("scoreT_ps"), sem("spread_done"), sem("pick_ps"), sem("pick_done"))
        slot_ps, slot_act, slot_dve = sem("slot_ps"), sem("slot_act"), sem("slot_dve")
        give_ps, give_done = sem("give_ps"), sem("give_done")
        sg_ps, sgelu_done, sh_done, sd_ps, sx_done = (
            sem("sg_ps"), sem("sgelu_done"), sem("sh_done"), sem("sd_ps"), sem("sx_done"))
        g_ps, u_ps, gelu_done, hid_done = sem("g_ps"), sem("u_ps"), sem("gelu_done"), sem("hid_done")
        hidT_ps, hidT_done, eo_ps, half_done, eo_done = (
            sem("hidT_ps"), sem("hidT_done"), sem("eo_ps"), sem("half_done"), sem("eo_done"))
        eo_sent = [sem(f"eo_sent{i}") for i in range(2)]
        y_ps, y_done, out_sent = sem("y_ps"), sem("y_done"), sem("out_sent")

        PROJ, TRANS, AV, SCORE = (0, 1), (2, 3), 4, (5, 6)
        LN_BANK, RES_BANK = (2, 4, 0), (0, 4)
        LIN_ORDER = [("k", 0), ("k", 1), ("kv", 0), ("k", 2), ("kv", 1), ("k", 3), ("kv", 2),
                     ("q", 0), ("kv", 3), ("q", 1), ("att", 0), ("q", 2), ("q", 3), ("att", 1)]
        QKV_BY = [("act",), ("dve",)] * 2 + [("act", "dve")] * 4 + [("act",), ("dve",)] * 2

        def qkv_count(n, who):
            return sum(who in by for by in QKV_BY[:n + 1])

        block = main.enter_context(nc.Block())

        @block.sync
        def _(sp):
            sp.dma_start(x[:], x_d.rearrange("(t p) d -> p t d", p=P)).then_inc(x_in, 16)
            sp.dma_start(ctx_raw[:], ctx_d[0]).then_inc(ctx_in, 16)
            sp.dma_start(k_T[:, 0], wk_d).then_inc(wk_in, 16)
            sp.dma_start(k_T[:, 1], wv_d).then_inc(wv_in, 16)
            for tile, src in ((bias_q, bq_d), (bias_k, bk_d), (bias_v, bv_d)):
                sp.dma_start(tile[:], src).then_inc(bias_in, 16)
            sp.dma_start(o_T[:], wq_d).then_inc(wq_in, 16)
            for i, src in enumerate((bo_d, bout_d)):
                sp.dma_start(row_bias[:, i, :], src.partition_broadcast(P)).then_inc(rows_in, 16)
            with sp.Fori(1, B) as b:
                sp.wait_ge(ctx_split, b)
                sp.dma_start(ctx_raw[:], ctx_d[b]).then_inc(ctx_in, 16)
            sp.dma_start(w_o[:], wo_d).then_inc(wo_in, 16)
            sp.dma_start(w_qkv[:], wqkv_d).then_inc(wqkv_in, 16)
            sp.wait_ge(x_done, NT)
            sp.dma_start(w_out[:], wout_d).then_inc(wout_in, 16)
            sp.wait_ge(vbd_zero, 2)
            for hh in range(HPT):
                rows = slice(HD * hh, HD * (hh + 1))
                sp.dma_start(proj[rows, :, hh, :], proj_d[:, rows, :].rearrange("t p f -> p t f")).then_inc(proj_in, 16)
            sp.wait_ge(x_done, 2 * NT)
            sp.dma_start(gate[:], gate_d).then_inc(gate_in, 16)
            for src, dst, s in ((wsg_d, w_g, wg_in), (wsu_d, w_u, wu_in), (wsd_d, w_d, wd_in)):
                sp.dma_start(dst[:, 0], src).then_inc(s[0], 16)
            for src, dst, s in ((wg_d, w_g, wg_in), (wu_d, w_u, wu_in), (wd_d, w_d, wd_in)):
                sp.dma_start(dst[:, 1], src[0]).then_inc(s[1], 16)

            def load_expert(e, buf, gu_used, d_used, uses):
                sp.wait_ge(gu_used, uses)
                sp.dma_start(w_g[:, buf], wg_d[e]).then_inc(wg_in[buf], 16)
                sp.dma_start(w_u[:, buf], wu_d[e]).then_inc(wu_in[buf], 16)
                sp.wait_ge(d_used, uses)
                sp.dma_start(w_d[:, buf], wd_d[e]).then_inc(wd_in[buf], 16)

            def send_expert(e, par):
                sp.wait_ge(eo_done, e + 1)
                for b in range(B):
                    rows = slice(CAP * b, CAP * (b + 1))
                    sp.dma_start(eo_slot[CAP * e:CAP * (e + 1), b, :], eo[rows, par, :]).then_inc(eo_sent[par], 16)

            load_expert(1, 0, sd_ps, sd_ps, NF)
            for e in range(E):
                if e + 2 < E:
                    load_expert(e + 2, (e + 1) % 2, u_ps, eo_ps, e + 1)
                send_expert(e, e % 2)
            for t in range(NT):
                sp.wait_ge(y_done, t + 1)
                sp.dma_start(out_d[P * t:P * (t + 1), :], x[:, t, :]).then_inc(out_sent, 16)
            sp.wait_ge(out_sent, 16 * NT)

        @block.gpsimd
        def _(pool):
            pool.memset(ident[:], 0.0).then_inc(consts, 1)
            pool.memset(ones[:], 1.0).then_inc(consts, 1)
            pool.memset(q_diag[:], 0.0).then_inc(consts, 1)
            pool.iota(iota_p[:], [[0, 1]], base=0, channel_multiplier=1,
                      allow_small_or_imprecise_dtypes=True).then_inc(consts, 1)
            pool.wait_ge(consts, 4)
            pool.affine_select(out=ident[:], in_=ident[:], compare_op=ALU.not_equal, fill=1.0, base=0,
                               pattern=[[-1, P]], channel_multiplier=1).then_inc(consts, 1)

            def build_diag(b):
                for hh in range(HPT):
                    rows = slice(HD * hh, HD * (hh + 1))
                    cols = slice(L * (hh % 2), L * (hh % 2 + 1))
                    pool.tensor_copy(q_diag[rows, :, hh // 2, cols],
                                     q_T[rows, :, bass.ds(b * L, L)]).then_inc(diag_done, 1)

            def add_row_bias(i):
                pool.wait_ge(xn_done, NT * (i + 1))
                for t in range(NT):
                    pool.tensor_tensor(x[:, t, :], x[:, t, :], row_bias[:, i, :], ALU.add).then_inc(xbias_done, 1)

            pool.wait_ge(q_done, KT)
            build_diag(0)
            pool.wait_ge(rows_in, 32)
            pool.wait_ge(diag_done, HPT)
            add_row_bias(0)
            pool.wait_ge(xbias_done, NT)
            with pool.Fori(1, B) as b:
                pool.wait_ge(score_ps, b * PAIRS)
                build_diag(b)

            pool.wait_ge(x_done, NT)
            pool.memset(proj[:], 0.0).then_inc(vbd_zero, 1)
            pool.memset(v_bd[:], 0.0).then_inc(vbd_zero, 1)
            pool.wait_ge(vbd_zero, 2)
            for par in range(2):
                rows = slice(L * par, L * (par + 1))
                pool.memset(v_bd[rows, :, :, par, HD:HD + 1], 1.0).then_inc(vbd_zero, 1)
            pool.wait_ge(vbd_zero, 4)
            add_row_bias(1)
            for u in range(2 * NT * KT):
                pool.wait_ge(fexp_done, u + 1)
                pool.tensor_scalar(exps[:, u % 4, :], exps[:, u % 4, :], 1.0, None, ALU.min).then_inc(fmin_done, 1)
            pool.wait_ge(x_done, 2 * NT)
            pool.memset(spread_i[:], 0.0).then_inc(consts, 1)
            pool.memset(spread_w[:], 0.0).then_inc(consts, 1)

        @block.scalar
        def _(act):
            def ln_std(k):
                act.wait_ge(stats_done, k + 1)
                act.activation(std[:], var_eps[:], ACT.Sqrt).then_inc(std_done, 1)

            def ln_copy(k):
                for dt in (0, 2):
                    act.wait_ge(xnT_ps, KT * k + dt + 1)
                    act.copy(xn_T[:, dt, :], bank(LN_BANK[k] + dt)).then_inc(xnT_act, 1)

            def ctx_high(b, par):
                act.wait_ge(ctx_in, (b + 1) * 16)
                act.copy(ctx_hi[:, par], ctx_raw[:]).then_inc(ctx_hi_done, 1)

            def v_out(b, par):
                for st in range(NS):
                    act.wait_ge(v_ps, b * NS + st + 1)
                    act.copy(v_s[:, par, st, :], bank(PROJ[st % 2])).then_inc(v_done, 1)

            def probs_T_out(b):
                for ht in range(KT):
                    act.wait_ge(pT_ps, b * PAIRS + 2 * ht + 1)
                    act.copy(probs_T[:, ht % 2, 0].rearrange("p s c -> p (s c)"), bank(TRANS[0])).then_inc(pT_done[0], 1)

            def exponents(b):
                for p in range(PAIRS):
                    act.wait_ge(max_done, b * PAIRS + p + 1)
                    act.activation(probs[:, p, :], bank(SCORE[p % 2]), ACT.Exp, bias=neg_max[:, p:p + 1], scale=1.0,
                                   accum_out=row_sum[:, p:p + 1]).then_inc(exp_done, 1)

            ln_std(0)
            act.wait_ge(wk_in, 16)
            act.copy(wk_hi[:], k_T[:, 0]).then_inc(w_hi, 1)
            ctx_high(0, 0)
            act.wait_ge(wv_in, 16)
            act.copy(wv_hi[:], k_T[:, 1]).then_inc(w_hi, 1)
            ln_copy(0)
            v_out(0, 0)
            ctx_high(1, 1)
            exponents(0)

            def step(b, par, more=True):
                if more:
                    ctx_high(b + 1, 1 - par)
                probs_T_out(b - 1)
                v_out(b, par)
                exponents(b)

            with act.Fori(1, B - 1, 2) as b:
                step(b, 1)
                step(b + 1, 0)
            step(B - 1, 1, more=False)
            probs_T_out(B - 1)

            ln_std(1)
            ln_copy(1)
            for n in range(12):
                if "act" not in QKV_BY[n]:
                    continue
                act.wait_ge(qkv_ps, n + 1)
                if n < 4:
                    act.copy(kl_T[:, n, :], bank(n % 4)).then_inc(qkv_act, 1)
                elif n < 8:
                    act.wait_ge(vbd_zero, 4)
                    act.copy(v_bd[0:L, n - 4, :, 0, 0:HD],
                             ps[0:L, n % 4, :].rearrange("p (h c) -> p h c", c=HD)).then_inc(qkv_act, 1)
                else:
                    act.copy(ql_T[:, n - 8, :], bank(n % 4)).then_inc(qkv_act, 1)
            u = w = 0
            for kind, i in LIN_ORDER:
                if kind in "kq":
                    for _ in range(4):
                        act.wait_ge(feat_ps, u + 1)
                        if u >= 4:
                            act.wait_ge(feat_done, u - 3)
                        act.activation(exps[:, u % 4, :], bank(u % 3), ACT.Exp).then_inc(fexp_done, 1)
                        u += 1
                elif kind == "kv":
                    for t in range(NT):
                        act.wait_ge(kv_ps, w + 1)
                        act.copy(kv[:, t, HPT * i:HPT * (i + 1), :],
                                 ps[:, 3 + w % 2, 0:HPT * 2 * KVW].rearrange("p (h c) -> p h c", h=HPT)).then_inc(kv_done, 1)
                        w += 1
            for dt in (0, 2):
                act.wait_ge(attT_ps, dt + 1)
                act.copy(att_T[:, dt, :], bank(dt)).then_inc(attT_act, 1)

            ln_std(2)
            ln_copy(2)
            act.wait_ge(lsub_done, 1)
            act.activation(logit[:], logit[:], ACT.Exp).then_inc(lexp_done, 1)
            for g in range(0, 2 * KT, 2):
                act.wait_ge(slot_ps, g + 1)
                act.copy(x_slot[:, g // 2, :, 0:32].rearrange("p e (t s) -> p t e s", t=2),
                         bank(2).rearrange("p (t e s) -> p t e s", t=2, e=E)).then_inc(slot_act, 1)
            for j in range(NF):
                act.wait_ge(sg_ps, 2 * j + 1)
                if j >= 2:
                    act.wait_ge(sh_done, j - 1)
                act.activation(gelu[:, j % 2, :], bank(4 + 2 * (j % 2)), ACT.Gelu).then_inc(sgelu_done, 1)

            def expert_gelu(e, par):
                act.wait_ge(g_ps, e + 1)
                act.activation(gelu[:, par, :], bank(2 * par), ACT.Gelu).then_inc(gelu_done, 1)

            def expert_out(e, par):
                act.wait_ge(hidT_ps, e + 1)
                act.copy(hid_T[:, par].rearrange("p j c -> p (j c)"), bank(4 + par)).then_inc(hidT_done, 1)
                act.wait_ge(eo_ps, e + 1)
                act.wait_ge(eo_done, e) if e else None
                act.copy(half[:, par, :], ps[SLOTS:P, 6 + par, :]).then_inc(half_done, 1)

            act.wait_ge(sh_done, NF)
            expert_gelu(0, 0)
            for e in range(1, E):
                expert_gelu(e, e % 2)
                expert_out(e - 1, (e - 1) % 2)
            expert_out(E - 1, (E - 1) % 2)

        @block.vector
        def _(dve):
            links = [0]

            def link(ins):
                links[0] += 1
                ins.then_inc(chain, 1)
                dve.wait_ge(chain, links[0])

            def ln_stats(k):
                for t in range(NT):
                    if k:
                        dve.wait_ge(x_done, NT * (k - 1) + t + 1)
                    ins = dve.bn_stats(stats[:, t, :], x[:, t, :])
                link(ins)
                for t in range(NT):
                    ins = dve.bn_aggr(mean_var[:, t, :], stats[:, t, :])
                link(ins)
                dve.tensor_scalar(var_eps[:], mean_var[:, :, 1], EPS, None, ALU.add).then_inc(stats_done, 1)

            def ln_rows(k, xn):
                dve.wait_ge(std_done, k + 1)
                link(dve.reciprocal(rstd[:], std[:]))
                link(dve.tensor_tensor(newton[:], rstd[:], rstd[:], ALU.mult))
                link(dve.tensor_tensor(newton[:], newton[:], var_eps[:], ALU.mult))
                link(dve.tensor_scalar(newton[:], newton[:], -0.5, 1.5, ALU.mult, ALU.add))
                link(dve.tensor_tensor(rstd[:], rstd[:], newton[:], ALU.mult))
                for t in range(NT):
                    dve.tensor_scalar(xn[:, t, :], x[:, t, :], mean_var[:, t, 0:1], rstd[:, t:t + 1],
                                      ALU.subtract, ALU.mult).then_inc(xn_done, 1)

            def ln_copy(k):
                for dt in (1, 3):
                    dve.wait_ge(xnT_ps, KT * k + dt + 1)
                    dve.tensor_copy(xn_T[:, dt, :], bank(LN_BANK[k] + dt)).then_inc(xnT_dve, 1)

            def ctx_low(b, par):
                dve.wait_ge(ctx_hi_done, b + 1)
                dve.tensor_tensor(ctx_lo[:, par], ctx_raw[:], ctx_hi[:, par].bitcast(F32),
                                  ALU.subtract).then_inc(ctx_split, 1)

            def w_low(n, lo, raw, hi):
                dve.wait_ge(w_hi, n)
                dve.tensor_tensor(lo[:], raw, hi[:].bitcast(F32), ALU.subtract).then_inc(w_split, 1)

            def k_out(b, par):
                for ht in range(KT):
                    dve.wait_ge(k_ps, b * KT + ht + 1)
                    dve.tensor_scalar(k_T[:, par, ht, :], bank(PROJ[ht % 2]), bias_k[:, ht:ht + 1], None,
                                      ALU.add).then_inc(k_done, 1)

            def probs_T_out(b):
                for ht in range(KT):
                    dve.wait_ge(pT_ps, b * PAIRS + 2 * ht + 2)
                    dve.tensor_copy(probs_T[:, ht % 2, 1].rearrange("p s c -> p (s c)"), bank(TRANS[1])).then_inc(pT_done[1], 1)

            def o_out(b):
                dve.wait_ge(o_ps, b * KT + KT)
                for hh in range(HPT):
                    rows = slice(HD * hh, HD * (hh + 1))
                    cols = slice(L * (hh % 2), L * (hh % 2 + 1))
                    dve.tensor_tensor(o_T[rows, :, bass.ds(b * L, L)],
                                      bank(AV).rearrange("p (t c) -> p t c", t=KT)[rows, :, cols],
                                      bias_v[rows, :].unsqueeze(2).to_broadcast([HD, KT, L]), ALU.add).then_inc(o_done, 1)

            def normalise(b, p):
                dve.wait_ge(exp_done, b * PAIRS + p + 1)
                dve.reciprocal(row_inv[:, p:p + 1], row_sum[:, p:p + 1]).then_inc(inv_done, 1)
                dve.wait_ge(inv_done, b * PAIRS + p + 1)
                dve.tensor_scalar(probs[:, p, :], probs[:, p, :], row_inv[:, p:p + 1], None,
                                  ALU.mult).then_inc(prob_done, 1)

            def softmax(b):
                for p in range(PAIRS):
                    dve.wait_ge(score_ps, b * PAIRS + p + 1)
                    dve.tensor_reduce(neg_max[:, p:p + 1], bank(SCORE[p % 2]), AX.X, ALU.max,
                                      negate=True).then_inc(max_done, 1)
                    if p:
                        normalise(b, p - 1)
                normalise(b, PAIRS - 1)

            dve.wait_ge(x_in, 16)
            ln_stats(0)
            w_low(1, wk_lo, k_T[:, 0], wk_hi)
            ctx_low(0, 0)
            w_low(2, wv_lo, k_T[:, 1], wv_hi)
            ln_rows(0, xn_cross)
            dve.wait_ge(bias_in, 48)
            dve.wait_ge(w_split, 2)
            k_out(0, 0)
            ln_copy(0)
            for ht in range(KT):
                dve.wait_ge(q_ps, ht + 1)
                dve.tensor_scalar(q_T[:, ht, :], bank(2 + ht), bias_q[:, ht:ht + 1], HD ** -0.5,
                                  ALU.add, ALU.mult).then_inc(q_done, 1)
            ctx_low(1, 1)
            softmax(0)

            def step(b, par, more=True):
                k_out(b, par)
                probs_T_out(b - 1)
                o_out(b - 1)
                if more:
                    ctx_low(b + 1, 1 - par)
                softmax(b)

            with dve.Fori(1, B - 1, 2) as b:
                step(b, 1)
                step(b + 1, 0)
            step(B - 1, 1, more=False)
            probs_T_out(B - 1)
            o_out(B - 1)

            def residual(k):
                for t in range(NT):
                    dve.wait_ge(xbias_done, NT * k + t + 1)
                    dve.wait_ge(res_ps, NT * k + t + 1)
                    dve.tensor_tensor(x[:, t, :], bank(RES_BANK[k] + t), x[:, t, :], ALU.add).then_inc(x_done, 1)

            residual(0)
            ln_stats(1)
            ln_rows(1, xn_lin)
            ln_copy(1)
            for n in range(12):
                if "dve" not in QKV_BY[n]:
                    continue
                dve.wait_ge(qkv_ps, n + 1)
                if n < 4:
                    dve.tensor_copy(kl_T[:, n, :], bank(n % 4)).then_inc(qkv_dve, 1)
                elif n < 8:
                    dve.wait_ge(vbd_zero, 4)
                    dve.tensor_copy(v_bd[L:P, n - 4, :, 1, 0:HD],
                                    ps[L:P, n % 4, :].rearrange("p (h c) -> p h c", c=HD)).then_inc(qkv_dve, 1)
                else:
                    dve.tensor_copy(ql_T[:, n - 8, :], bank(n % 4)).then_inc(qkv_dve, 1)
            u = a = 0
            for kind, i in LIN_ORDER:
                if kind in "kq":
                    for r in range(4):
                        dve.wait_ge(fmin_done, u + 1)
                        dst = k_feat[:, i % 2, r, :] if kind == "k" else q_feat[:, 4 * i + r, :]
                        if kind == "k" and i >= 2:
                            dve.wait_ge(kv_ps, NT * (i - 1))
                        dve.scalar_tensor_tensor(out=dst, in0=bank(u % 3), scalar=0.0, in1=exps[:, u % 4, :],
                                                 op0=ALU.max, op1=ALU.add).then_inc(feat_done, 1)
                        u += 1
                elif kind == "att":
                    for t in range(NT):
                        dve.wait_ge(att_ps, a + 1)
                        got = ps[:, 5 + a % 2, 0:8 * (HD + 1)].rearrange("p (h c) -> p h c", h=8)
                        link(dve.tensor_scalar(den[:, a, :], got[:, :, HD], 1e-8, None, ALU.add))
                        link(dve.reciprocal(den_inv[:, a, :], den[:, a, :]))
                        dve.tensor_tensor(att[:, t, 256 * i:256 * (i + 1)].rearrange("p (h c) -> p h c", h=8),
                                          got[:, :, 0:HD], den_inv[:, a, :].unsqueeze(2).to_broadcast([P, 8, HD]),
                                          ALU.mult).then_inc(att_done, 1)
                        a += 1
            for dt in (1, 3):
                dve.wait_ge(attT_ps, dt + 1)
                dve.tensor_copy(att_T[:, dt, :], bank(dt)).then_inc(attT_dve, 1)
            residual(1)
            ln_stats(2)
            ln_rows(2, xn_moe)
            ln_copy(2)

            def over_experts(v):
                return v[:].unsqueeze(2).to_broadcast([P, NT, E])

            dve.wait_ge(logit_ps, 1)
            got = ps[:, 4, 0:NT * LGW].rearrange("p (t c) -> p t c", t=NT)[:, :, 0:E]
            link(dve.tensor_reduce(lmax[:], got, AX.X, ALU.max))
            dve.tensor_tensor(logit[:], got, over_experts(lmax), ALU.subtract).then_inc(lsub_done, 1)
            dve.wait_ge(lexp_done, 1)
            link(dve.tensor_reduce(lsum[:], logit[:], AX.X, ALU.add))
            link(dve.reciprocal(linv[:], lsum[:]))
            dve.tensor_tensor(logit[:], logit[:], over_experts(linv), ALU.mult).then_inc(score_done, 1)
            dve.wait_ge(scoreT_ps, 1)
            link(dve.tensor_copy(score_T[:], ps[0:E, 5, :]))
            for b in range(B):
                ins = dve.max(top_w[:, b, :], score_T[:, L * b:L * (b + 1)])
            link(ins)
            for b in range(B):
                ins = dve.max_index(top_i[:, b, :], top_w[:, b, :], score_T[:, L * b:L * (b + 1)])
            link(ins)
            link(dve.tensor_copy(top_f[:], top_i[:]))
            odd = top_f[:].rearrange("e (t u) c -> e t u c", u=2)[:, :, 1, :]
            link(dve.tensor_scalar(odd, odd, float(L), None, ALU.add))
            dve.wait_ge(consts, 7)
            own = ident[0:E, 0:E].unsqueeze(2).to_broadcast([E, E, SLOTS])
            for src, dst in ((top_f, spread_i), (top_w, spread_w)):
                flat = src[:].rearrange("e b c -> e (b c)").unsqueeze(1).to_broadcast([E, E, SLOTS])
                dve.tensor_tensor(dst[0:E], flat, own, ALU.mult).then_inc(spread_done, 1)
            pick2 = pick[:].rearrange("p e s -> p (e s)")
            for i in range(2):
                dve.wait_ge(pick_ps, i + 1)
                cols = slice(BANK * i, BANK * (i + 1))
                dve.tensor_scalar(pick2[:, cols], bank(6 + i), iota_p[:, 0:1], None, ALU.is_equal).then_inc(pick_done, 1)
            dve.wait_ge(pick_done, 2)
            for i in range(2):
                dve.wait_ge(pick_ps, i + 3)
                cols = slice(BANK * i, BANK * (i + 1))
                half_e = slice(E // 2 * i, E // 2 * (i + 1))
                dve.tensor_tensor(pick_w[:, :, half_e, :].rearrange("p b e c -> p e b c"),
                                  pick[:, half_e, :].rearrange("p e (b c) -> p e b c", b=B),
                                  bank(i).rearrange("p (e b c) -> p e b c", e=E // 2, b=B), ALU.mult).then_inc(pick_done, 1)
            for g in range(1, 2 * KT, 2):
                dve.wait_ge(slot_ps, g + 1)
                dve.tensor_copy(x_slot[:, g // 2, :, 32:64].rearrange("p e (t s) -> p t e s", t=2),
                                bank(3).rearrange("p (t e s) -> p t e s", t=2, e=E)).then_inc(slot_dve, 1)
            for i in range(2):
                dve.wait_ge(give_ps, i + 1)
                for par in range(2):
                    src = bank(4 + i).rearrange("p (b u l) -> p b u l", u=2, l=L).rearrange(
                        "p (t v) u l -> p t v u l", v=2)[:, :, par, par, :]
                    dst = give[:, 4 * i:4 * (i + 1), :].rearrange("p (t v) l -> p t v l", v=2)[:, :, par, :]
                    dve.tensor_copy(dst, src).then_inc(give_done, 1)
            for j in range(NF):
                dve.wait_ge(sgelu_done, j + 1)
                dve.wait_ge(sg_ps, 2 * j + 2)
                if j >= 2:
                    dve.wait_ge(sd_ps, j - 1)
                dve.tensor_tensor(hid[:, j % 2, :], gelu[:, j % 2, :], bank(5 + 2 * (j % 2)), ALU.mult).then_inc(sh_done, 1)
            dve.wait_ge(sd_ps, NF)
            for t in range(NT):
                dve.tensor_tensor(x[:, t, :], bank(t), x[:, t, :], ALU.add).then_inc(sx_done, 1)

            def expert_hidden(e, par):
                dve.wait_ge(gelu_done, e + 1)
                dve.wait_ge(u_ps, e + 1)
                dve.tensor_tensor(hid[:, par, :], gelu[:, par, :], bank(2 * par + 1), ALU.mult).then_inc(hid_done, 1)

            def expert_sum(e, par):
                dve.wait_ge(half_done, e + 1)
                if e >= 2:
                    dve.wait_ge(eo_sent[par], 16 * B * (e // 2))
                dve.tensor_tensor(eo[:, par, :], ps[0:SLOTS, 6 + par, :], half[:, par, :], ALU.add).then_inc(eo_done, 1)

            expert_hidden(0, 0)
            for e in range(1, E):
                expert_hidden(e, e % 2)
                expert_sum(e - 1, (e - 1) % 2)
            expert_sum(E - 1, (E - 1) % 2)
            dve.wait_ge(sx_done, NT)
            for t in range(NT):
                dve.wait_ge(y_ps, t + 1)
                dve.tensor_tensor(x[:, t, :], bank(t), x[:, t, :], ALU.add).then_inc(y_done, 1)

        @block.tensor
        def _(pe):
            def ln_transpose(k, xn):
                for t in range(NT):
                    pe.wait_ge(xn_done, NT * k + t + 1)
                    for dt in range(KT):
                        ins = pe.transpose(ps[:, LN_BANK[k] + dt, P * t:P * (t + 1)], xn[:, t, P * dt:P * (dt + 1)],
                                           ident[:])
                        if t == NT - 1:
                            ins.then_inc(xnT_ps, 1)

            def xn_T_ready(k):
                pe.wait_ge(xnT_act, 2 * (k + 1))
                pe.wait_ge(xnT_dve, 2 * (k + 1))

            def product3(dst, lhs, rhs):
                (l_hi, l_lo), (r_hi, r_lo) = lhs, rhs
                for dt in range(KT):
                    for i, (a, c) in enumerate(((l_hi, r_hi), (l_hi, r_lo), (l_lo, r_hi))):
                        ins = pe.matmul(dst, a(dt), c(dt), start=(dt == 0 and i == 0), stop=(dt == KT - 1 and i == 2))
                return ins

            def project_k(b, par, first=False):
                pe.wait_ge(ctx_split, b + 1)
                for ht in range(KT):
                    if ht >= 2:
                        pe.wait_ge(k_done, b * KT + ht - 1)
                    elif not first:
                        pe.wait_ge(v_done, b * NS + ht - 1)
                    cols = slice(P * ht, P * (ht + 1))
                    product3(bank(PROJ[ht % 2]),
                             (lambda dt: wk_hi[:, dt, cols], lambda dt: wk_lo[:, dt, cols]),
                             (lambda dt: ctx_hi[:, par, dt, :], lambda dt: ctx_lo[:, par, dt, :])).then_inc(k_ps, 1)

            def project_v(b, par):
                for st in range(NS):
                    if st >= 2:
                        pe.wait_ge(v_done, b * NS + st - 1)
                    else:
                        pe.wait_ge(k_done, b * KT + st + 3)
                    cols = slice(P * st, P * (st + 1))
                    product3(bank(PROJ[st % 2]),
                             (lambda dt: ctx_hi[:, par, dt, cols], lambda dt: ctx_lo[:, par, dt, cols]),
                             (lambda dt: wv_hi[:, dt, :], lambda dt: wv_lo[:, dt, :])).then_inc(v_ps, 1)

            def scores(b, par, first=False):
                pe.wait_ge(diag_done, b * HPT + HPT)
                for p in range(PAIRS):
                    if p % 2 == 0:
                        pe.wait_ge(k_done, b * KT + p // 2 + 1)
                    if not (first and p < 2):
                        pe.wait_ge(exp_done, b * PAIRS + p - 1)
                    pe.matmul(bank(SCORE[p % 2]), q_diag[:, p // 2, p % 2, :], k_T[:, par, p // 2, :],
                              start=True, stop=True).then_inc(score_ps, 1)

            def probs_transpose(b, ht):
                for pr in range(2):
                    pe.wait_ge(prob_done, b * PAIRS + 2 * ht + pr + 1)
                    if ht:
                        pe.wait_ge(pT_done[pr], b * KT + ht)
                    for st in range(NS):
                        ins = pe.transpose(ps[:, TRANS[pr], P * st:P * (st + 1)],
                                           probs[:, 2 * ht + pr, P * st:P * (st + 1)], ident[:])
                    ins.then_inc(pT_ps, 1)

            def attend(b, par, ht):
                for pr in range(2):
                    pe.wait_ge(pT_done[pr], b * KT + ht + 1)
                for st in range(NS):
                    for pr in range(2):
                        cols = slice(2 * HD * (2 * ht + pr), 2 * HD * (2 * ht + pr + 1))
                        ins = pe.matmul(ps[64 * pr:64 * (pr + 1), AV, P * ht:P * (ht + 1)], v_s[:, par, st, cols],
                                        probs_T[:, ht % 2, pr, st, :], start=(st == 0), stop=(st == NS - 1),
                                        skip_group_check=True)
                ins.then_inc(o_ps, 1)

            def attention(b, par):
                pe.wait_ge(v_done, b * NS + NS)
                probs_transpose(b, 0)
                for ht in range(1, KT):
                    probs_transpose(b, ht)
                    attend(b, par, ht - 1)
                attend(b, par, KT - 1)

            pe.wait_ge(consts, 5)
            ln_transpose(0, xn_cross)
            pe.wait_ge(w_split, 1)
            project_k(0, 0, first=True)
            pe.wait_ge(w_split, 2)
            project_v(0, 0)
            xn_T_ready(0)
            pe.wait_ge(wq_in, 16)
            for ht in range(KT):
                for dt in range(KT):
                    ins = pe.matmul(bank(2 + ht), o_T[:, dt, P * ht:P * (ht + 1)], xn_T[:, dt, :],
                                    start=(dt == 0), stop=(dt == KT - 1))
                ins.then_inc(q_ps, 1)
            scores(0, 0, first=True)

            def step(b, par):
                project_k(b, par)
                attention(b - 1, 1 - par)
                project_v(b, par)
                scores(b, par)

            with pe.Fori(1, B - 1, 2) as b:
                step(b, 1)
                step(b + 1, 0)
            step(B - 1, 1)
            attention(B - 1, 1)

            def residual(k, rows_T, w):
                for t in range(NT):
                    for dt in range(KT):
                        ins = pe.matmul(bank(RES_BANK[k] + t), rows_T[:, dt, P * t:P * (t + 1)], w[:, dt, :],
                                        start=(dt == 0), stop=(dt == KT - 1))
                    ins.then_inc(res_ps, 1)

            pe.wait_ge(o_done, B * HPT)
            pe.wait_ge(wo_in, 16)
            residual(0, o_T, w_o)

            ln_transpose(1, xn_lin)
            xn_T_ready(1)
            pe.wait_ge(wqkv_in, 16)

            def qkv_out(n):
                if "act" in QKV_BY[n]:
                    pe.wait_ge(qkv_act, qkv_count(n, "act"))
                if "dve" in QKV_BY[n]:
                    pe.wait_ge(qkv_dve, qkv_count(n, "dve"))

            for n in range(12):
                if n >= 4:
                    qkv_out(n - 4)
                for dt in range(KT):
                    if 4 <= n < 8:
                        t = n - 4
                        a, c = xn_T[:, dt, P * t:P * (t + 1)], w_qkv[:, dt, 2 * D:3 * D]
                    else:
                        at = D + P * n if n < 4 else P * (n - 8)
                        a, c = w_qkv[:, dt, at:at + P], xn_T[:, dt, :]
                    ins = pe.matmul(bank(n % 4), a, c, start=(dt == 0), stop=(dt == KT - 1))
                ins.then_inc(qkv_ps, 1)
            pe.wait_ge(proj_in, 64)
            for n in range(8, 12):
                qkv_out(n)

            u = w = a = 0
            for kind, i in LIN_ORDER:
                if kind in "kq":
                    for r in range(4):
                        if u >= 3:
                            pe.wait_ge(feat_done, u - 2)
                        if kind == "k":
                            lhs, rhs = kl_T[:, i, P * r:P * (r + 1)], proj[:, i].rearrange("p h f -> p (h f)")
                        else:
                            lhs, rhs = proj[:, i, r, :], ql_T[:, i, :]
                        pe.matmul(bank(u % 3), lhs, rhs, start=True, stop=True).then_inc(feat_ps, 1)
                        u += 1
                elif kind == "kv":
                    for t in range(NT):
                        pe.wait_ge(feat_done, (4 * i + t if i < 4 else 0) + 1)
                        if w >= 2:
                            pe.wait_ge(kv_done, w - 1)
                        for hh in range(HPT):
                            ins = pe.matmul(ps[:, 3 + w % 2, 2 * KVW * hh:2 * KVW * (hh + 1)],
                                            k_feat[:, i % 2, t, FEAT * hh:FEAT * (hh + 1)],
                                            v_bd[:, t, HPT * i + hh].rearrange("p u c -> p (u c)"), start=True, stop=True)
                        ins.then_inc(kv_ps, 1)
                        w += 1
                else:
                    pe.wait_ge(kv_done, 8 * (i + 1))
                    pe.wait_ge(feat_done, 16 + 8 * (i + 1))
                    for t in range(NT):
                        if a >= 2:
                            pe.wait_ge(att_done, a - 1)
                        for h in range(8):
                            for par in range(2):
                                b = 2 * t + par
                                ins = pe.matmul(ps[L * par:L * (par + 1), 5 + a % 2, (HD + 1) * h:(HD + 1) * (h + 1)],
                                                q_feat[:, 8 * i + h, L * b:L * (b + 1)],
                                                kv[:, t, 8 * i + h, KVW * par:KVW * par + HD + 1],
                                                start=True, stop=True, skip_group_check=True)
                        ins.then_inc(att_ps, 1)
                        a += 1
            pe.wait_ge(feat_done, 32)
            for t in range(NT):
                pe.wait_ge(att_done, NT + t + 1)
                for dt in range(KT):
                    ins = pe.transpose(ps[:, dt, P * t:P * (t + 1)], att[:, t, P * dt:P * (dt + 1)], ident[:])
                    if t == NT - 1:
                        ins.then_inc(attT_ps, 1)
            pe.wait_ge(attT_act, 2)
            pe.wait_ge(attT_dve, 2)
            pe.wait_ge(wout_in, 16)
            residual(1, att_T, w_out)

            ln_transpose(2, xn_moe)
            xn_T_ready(2)
            pe.wait_ge(gate_in, 16)
            for t in range(NT):
                for dt in range(KT):
                    ins = pe.matmul(ps[:, 4, LGW * t:LGW * (t + 1)], xn_T[:, dt, P * t:P * (t + 1)], gate[:, dt, :],
                                    start=(dt == 0), stop=(dt == KT - 1))
            ins.then_inc(logit_ps, 1)
            pe.wait_ge(score_done, 1)
            for t in range(NT):
                ins = pe.transpose(ps[0:E, 5, P * t:P * (t + 1)], logit[:, t, :], ident[:])
            ins.then_inc(scoreT_ps, 1)
            for k, (src, first) in enumerate(((spread_i, 6), (spread_w, 0))):
                pe.wait_ge(spread_done, k + 1)
                for i in range(2):
                    pe.matmul(bank(first + i), ones[:], src[:].rearrange("p e s -> p (e s)")[:, BANK * i:BANK * (i + 1)],
                              start=True, stop=True).then_inc(pick_ps, 1)
            pe.wait_ge(pick_done, 2)
            for g in range(2 * KT):
                if g >= 2:
                    pe.wait_ge(slot_dve if g % 2 else slot_act, g // 2)
                for i in range(2):
                    t = 2 * (g % 2) + i
                    ins = pe.matmul(ps[:, 2 + g % 2, 256 * i:256 * (i + 1)], xn_moe[:, t, P * (g // 2):P * (g // 2 + 1)],
                                    pick[:, :, 2 * CAP * t:2 * CAP * (t + 1)], start=True, stop=True)
                ins.then_inc(slot_ps, 1)
            pe.wait_ge(pick_done, 4)
            for b in range(B):
                ins = pe.transpose(ps[:, 4 + b // 4, P * (b % 4):P * (b % 4 + 1)],
                                   pick_w[:, b].rearrange("p e c -> p (e c)"), ident[:])
                if b % 4 == 3:
                    ins.then_inc(give_ps, 1)

            def shared_up(j):
                if j >= 2:
                    pe.wait_ge(sh_done, j - 1)
                for w, off in ((w_g, 4), (w_u, 5)):
                    for dt in range(KT):
                        ins = pe.matmul(bank(off + 2 * (j % 2)), w[:, 0, dt, P * j:P * (j + 1)], xn_T[:, dt, :],
                                        start=(dt == 0), stop=(dt == KT - 1))
                    ins.then_inc(sg_ps, 1)

            def shared_down(j):
                pe.wait_ge(sh_done, j + 1)
                for t in range(NT):
                    ins = pe.matmul(bank(t), hid[:, j % 2, P * t:P * (t + 1)], w_d[:, 0, j, :],
                                    start=(j == 0), stop=(j == NF - 1))
                ins.then_inc(sd_ps, 1)

            pe.wait_ge(give_done, 4)
            pe.wait_ge(slot_act, KT)
            pe.wait_ge(slot_dve, KT)
            pe.wait_ge(wg_in[0], 16)
            pe.wait_ge(wu_in[0], 16)
            shared_up(0)
            pe.wait_ge(wd_in[0], 16)
            for j in range(1, NF):
                shared_up(j)
                shared_down(j - 1)
            shared_down(NF - 1)

            def expert_up(e, par, w, off, in_, done):
                pe.wait_ge(in_[1 - par], 16 * ((e + 1) // 2 + 1))
                for dt in range(KT):
                    for fh in range(2):
                        ins = pe.matmul(ps[64 * fh:64 * (fh + 1), 2 * par + off, :], x_slot[:, dt, e, :],
                                        w[:, 1 - par, dt, BANK * fh:BANK * (fh + 1)],
                                        start=(dt == 0), stop=(dt == KT - 1), skip_group_check=True)
                ins.then_inc(done, 1)

            def expert_transpose(e, par):
                pe.wait_ge(hid_done, e + 1)
                for j in range(KT):
                    ins = pe.transpose(ps[:, 4 + par, P * j:P * (j + 1)], hid[:, par, P * j:P * (j + 1)], ident[:])
                ins.then_inc(hidT_ps, 1)

            def expert_down(e, par):
                pe.wait_ge(hidT_done, e + 1)
                pe.wait_ge(wd_in[1 - par], 16 * ((e + 1) // 2 + 1))
                for j in range(KT):
                    for fh in range(2):
                        ins = pe.matmul(ps[64 * fh:64 * (fh + 1), 6 + par, :], hid_T[:, par, j, 64 * fh:64 * (fh + 1)],
                                        w_d[:, 1 - par, KT * fh + j, :], start=(j == 0), stop=(j == KT - 1),
                                        skip_group_check=True)
                ins.then_inc(eo_ps, 1)

            pe.wait_ge(sx_done, NT)
            expert_up(0, 0, w_g, 0, wg_in, g_ps)
            expert_up(0, 0, w_u, 1, wu_in, u_ps)
            for e in range(1, E):
                expert_up(e, e % 2, w_g, 0, wg_in, g_ps)
                expert_transpose(e - 1, (e - 1) % 2)
                expert_up(e, e % 2, w_u, 1, wu_in, u_ps)
                expert_down(e - 1, (e - 1) % 2)
            expert_transpose(E - 1, 1)
            expert_down(E - 1, 1)
            pe.wait_ge(eo_sent[0], 16 * B * E // 2)
            pe.wait_ge(eo_sent[1], 16 * B * E // 2)
            for b in range(B):
                rows = slice(L * (b % 2), L * (b % 2 + 1))
                ins = pe.matmul(ps[rows, b // 2, :], give[:, b, :], eo_slot[:, b, :], start=True, stop=True,
                                skip_group_check=True)
                if b % 2:
                    ins.then_inc(y_ps, 1)


def rows_first(w, tiles):
    return np.ascontiguousarray(w.reshape(*w.shape[:-2], tiles, P, w.shape[-1]).swapaxes(-3, -2))


def kernel(**inputs):
    import concourse.bacc as bacc
    from concourse.bass_utils import run_bass_kernel_spmd

    a = {k: np.asarray(v) for k, v in inputs.items()}
    gate = np.zeros((D, LGW), np.float32)
    gate[:, :E] = a["L0_ffn_gate_w"].T
    arrays = {
        "x": np.ascontiguousarray(a["x"].reshape(TOK, D)),
        "ctx": rows_first(a["ctx_1024"].swapaxes(1, 2), KT),
        "wq": rows_first(a["L0_xattn_Wq"], KT),
        "bq": np.ascontiguousarray(a["L0_xattn_bq"].reshape(KT, P).T),
        "wk": rows_first(a["L0_xattn_Wk"], KT),
        "bk": np.ascontiguousarray(a["L0_xattn_bk"].reshape(KT, P).T),
        "wv": rows_first(a["L0_xattn_Wv"], KT),
        "bv": np.ascontiguousarray(a["L0_xattn_bv"].reshape(KT, P).T),
        "wo": rows_first(a["L0_xattn_Wo"], KT),
        "bo": a["L0_xattn_bo"],
        "wqkv": rows_first(a["L0_attn_w_qkv"], KT),
        "proj": np.ascontiguousarray(a["L0_attn_proj_matrix"].reshape(KT, HPT * HD, FEAT)),
        "wout": rows_first(a["L0_attn_w_out"], KT),
        "bout": a["L0_attn_b_out"],
        "gate": rows_first(gate, KT),
        "wg": rows_first(a["L0_ffn_Wg"].swapaxes(1, 2), KT),
        "wu": rows_first(a["L0_ffn_Wu"].swapaxes(1, 2), KT),
        "wd": rows_first(a["L0_ffn_Wd"].swapaxes(1, 2), NF),
        "wsg": rows_first(a["L0_ffn_Ws_g"].T, KT),
        "wsu": rows_first(a["L0_ffn_Ws_u"].T, KT),
        "wsd": rows_first(a["L0_ffn_Ws_d"].T, NF),
    }
    nc = bacc.Bacc("TRN2", target_bir_lowering=False, num_devices=1)
    args = [nc.dram_tensor(f"in_{k}", v.shape, mybir.dt.from_np(v.dtype), kind="ExternalInput").ap() for k, v in arrays.items()]
    out = nc.dram_tensor("out", (TOK, D), F32, kind="ExternalOutput").ap()
    perceiver_block(nc, *args, out)
    r = run_bass_kernel_spmd(nc, [{f"in_{k}": v for k, v in arrays.items()}], core_ids=[0])
    return r.results[0]["out"].reshape(B, L, D)
```

```python
from contextlib import ExitStack

import numpy as np

import concourse.bass as bass
from concourse import mybir

F32 = mybir.dt.float32
F32R = mybir.dt.float32r
U32 = mybir.dt.uint32
ALU = mybir.AluOpType
ACT = mybir.ActivationFunctionType
AX = mybir.AxisListType

P = 128
B, L, S, D = 8, 64, 512, 512
H, HD, FEAT = 16, 32, 128
E, CAP, FF = 16, 8, 1024
TOK = B * L
NT = TOK // P
KT = D // P
NS = S // P
NF = FF // P
HPT = P // HD
PAIRS = H // 2
SLOTS = B * CAP
KVW = 48
LGW = 96
EPS = 1e-5
BANK = 512


def perceiver_block(nc, x_d, ctx_d, wq_d, bq_d, wk_d, bk_d, wv_d, bv_d, wo_d, bo_d, wqkv_d, proj_d,
                    wout_d, bout_d, gate_d, wg_d, wu_d, wd_d, wsg_d, wsu_d, wsd_d, out_d):
    main = ExitStack()
    with main:
        def sb(stack, name, shape, dt=F32):
            return stack.enter_context(nc.sbuf_tensor(name, shape, dt))

        def sem(name):
            return main.enter_context(nc.semaphore(name))

        x = sb(main, "x", [P, NT, D])
        xn_T = sb(main, "xn_T", [P, KT, TOK])
        ident = sb(main, "ident", [P, P])
        iota_p = sb(main, "iota_p", [P, 1])
        ones = sb(main, "ones", [P, P])
        bias_q = sb(main, "bias_q", [P, KT])
        bias_k = sb(main, "bias_k", [P, KT])
        bias_v = sb(main, "bias_v", [P, KT])
        stats = sb(main, "stats", [P, NT, 6])
        mean_var = sb(main, "mean_var", [P, NT, 2])
        var_eps = sb(main, "var_eps", [P, NT])
        std = sb(main, "std", [P, NT])
        rstd = sb(main, "rstd", [P, NT])
        newton = sb(main, "newton", [P, NT])

        early = ExitStack()
        w_qkv = sb(early, "w_qkv", [P, KT, 3 * D])
        w_o = sb(early, "w_o", [P, KT, D])
        cross = ExitStack()
        bo_rows = sb(cross, "bo_rows", [P, D])
        q_T = sb(cross, "q_T", [P, KT, TOK])
        wk_hi = sb(cross, "wk_hi", [P, KT, D], F32R)
        wk_lo = sb(cross, "wk_lo", [P, KT, D], F32R)
        wv_hi = sb(cross, "wv_hi", [P, KT, D], F32R)
        wv_lo = sb(cross, "wv_lo", [P, KT, D], F32R)
        ctx_raw = sb(cross, "ctx_raw", [P, KT, S])
        ctx_hi = sb(cross, "ctx_hi", [P, 2, KT, S], F32R)
        ctx_lo = sb(cross, "ctx_lo", [P, 2, KT, S], F32R)
        k_T = sb(cross, "k_T", [P, 2, KT, S])
        v_s = sb(cross, "v_s", [P, 2, NS, D])
        probs = sb(cross, "probs", [P, PAIRS, S])
        probs_T = sb(cross, "probs_T", [P, 2, 2, NS, P])
        q_diag = sb(cross, "q_diag", [P, KT, 2, P])
        o_T = sb(cross, "o_T", [P, KT, TOK])
        neg_max = sb(cross, "neg_max", [P, PAIRS])
        row_sum = sb(cross, "row_sum", [P, PAIRS])
        row_inv = sb(cross, "row_inv", [P, PAIRS])
        cross.close()
        xn_cross = probs
        linear = ExitStack()
        kl_T = sb(linear, "kl_T", [P, KT, TOK])
        k_feat = sb(linear, "k_feat", [P, 2, NT, HPT * FEAT])
        v_bd = sb(linear, "v_bd", [P, NT, H, 2, KVW])
        w_out = sb(linear, "w_out", [P, KT, D])
        bout_rows = sb(linear, "bout_rows", [P, D])
        xn_lin = sb(linear, "xn_lin", [P, NT, D])
        ql_T = sb(linear, "ql_T", [P, KT, TOK])
        proj = sb(linear, "proj", [P, KT, HPT, FEAT])
        q_feat = sb(linear, "q_feat", [P, H, TOK])
        kv = sb(linear, "kv", [P, NT, H, 2 * KVW])
        relus = sb(linear, "relus", [P, 2, BANK])
        exps = sb(linear, "exps", [P, 4, BANK])
        den = sb(linear, "den", [P, 8, 8])
        den_inv = sb(linear, "den_inv", [P, 8, 8])
        linear.close()
        early.close()
        att = xn_lin
        att_T = ql_T
        moe = ExitStack()
        ws_g = sb(moe, "ws_g", [P, KT, FF])
        ws_u = sb(moe, "ws_u", [P, KT, FF])
        w_u0 = sb(moe, "w_u0", [P, KT, FF])
        w_d0 = sb(moe, "w_d0", [P, NF, D])
        ws_d = sb(moe, "ws_d", [P, NF, D])
        w_g0 = sb(moe, "w_g0", [P, KT, FF])
        w_g1 = sb(moe, "w_g1", [P, KT, FF])
        w_u1 = sb(moe, "w_u1", [P, KT, FF])
        w_d1 = sb(moe, "w_d1", [P, NF, D])
        w_g, w_u, w_d = (w_g0, w_g1), (w_u0, w_u1), (w_d0, w_d1)
        x_slot = sb(moe, "x_slot", [P, KT, E, SLOTS])
        give = sb(moe, "give", [P, B, L])
        router = ExitStack()
        gate = sb(router, "gate", [P, KT, LGW])
        router.close()
        eo = sb(moe, "eo", [P, D])
        route = ExitStack()
        xn_moe = sb(route, "xn_moe", [P, NT, D])
        pick = sb(route, "pick", [P, E, SLOTS])
        spread_i = sb(route, "spread_i", [P, E, SLOTS])
        route.close()
        eo_slot = sb(moe, "eo_slot", [P, B, D])
        hid = sb(moe, "hid", [P, 2, BANK])
        late = ExitStack()
        spread_w = sb(late, "spread_w", [P, E, SLOTS])
        late.close()
        hid_T = sb(moe, "hid_T", [P, 2, KT, P])
        pick_w = spread_i[:].rearrange("p e s -> p (e s)").rearrange("p (b e c) -> p b e c", b=B, e=E)
        logit = sb(moe, "logit", [P, NT, E])
        lmax = sb(moe, "lmax", [P, NT])
        lsum = sb(moe, "lsum", [P, NT])
        linv = sb(moe, "linv", [P, NT])
        top_w = sb(moe, "top_w", [E, B, CAP])
        top_i = sb(moe, "top_i", [E, B, CAP], U32)
        top_f = sb(moe, "top_f", [E, B, CAP])
        score_T = give[:].rearrange("p b l -> p (b l)")[0:E]
        moe.close()

        ps = main.enter_context(nc.psum_tensor("ps", [P, 8, BANK], F32))

        def bank(n):
            return ps[:, n, :]

        x_in, wq_in, wv_in, bias_in = (sem(f"{n}_in") for n in ("x", "wq", "wv", "bias"))
        wk_in = [sem(f"wk_in{dt}") for dt in range(KT)]
        ctx0_in = [sem(f"ctx0_in{dt}") for dt in range(KT)]
        ctx_in, wqkv_in, wo_in, wout_in, rows_in = (sem(f"{n}_in") for n in ("ctx", "wqkv", "wo", "wout", "rows"))
        proj_in, gate_in = sem("proj_in"), sem("gate_in")
        wg_in, wu_in, wd_in = ([sem(f"{n}_in{i}") for i in range(2)] for n in ("wg", "wu", "wd"))
        wsg_in, wsu_in, wsd_in = sem("wsg_in"), sem("wsu_in"), sem("wsd_in")
        consts = sem("consts")
        chain = sem("dve_chain")
        stats_done, std_done, xn_done = sem("stats_done"), sem("std_done"), sem("xn_done")
        xnT_ps, xnT_act, xnT_dve = sem("xnT_ps"), sem("xnT_act"), sem("xnT_dve")
        w_hi, w_split = sem("w_hi"), sem("w_split")
        ctx_hi_done, ctx_split = sem("ctx_hi_done"), sem("ctx_split")
        k_ps, k_done, v_ps, v_done = sem("k_ps"), sem("k_done"), sem("v_ps"), sem("v_done")
        q_ps, q_done, diag_done = sem("q_ps"), sem("q_done"), sem("diag_done")
        score_ps, max_done, exp_done, inv_done, prob_done = (
            sem("score_ps"), sem("max_done"), sem("exp_done"), sem("inv_done"), sem("prob_done"))
        pT_ps = sem("pT_ps")
        pT_done = [sem("pT_done_act"), sem("pT_done_dve")]
        o_ps, o_done = sem("o_ps"), sem("o_done")
        xbias_done, res_ps, x_done = sem("xbias_done"), sem("res_ps"), sem("x_done")
        qkv_ps, qkv_act, qkv_dve = sem("qkv_ps"), sem("qkv_act"), sem("qkv_dve")
        vbd_zero = sem("vbd_zero")
        feat_ps, fexp_done, frelu_done, feat_done = (
            sem("feat_ps"), sem("fexp_done"), sem("frelu_done"), sem("feat_done"))
        kv_ps, kv_done, att_ps, att_done = sem("kv_ps"), sem("kv_done"), sem("att_ps"), sem("att_done")
        attT_ps, attT_act, attT_dve = sem("attT_ps"), sem("attT_act"), sem("attT_dve")
        logit_ps, lsub_done, lexp_done, score_done = (
            sem("logit_ps"), sem("lsub_done"), sem("lexp_done"), sem("score_done"))
        scoreT_ps, spread_done, pick_ps, pick_done = (
            sem("scoreT_ps"), sem("spread_done"), sem("pick_ps"), sem("pick_done"))
        slot_ps, slot_act, slot_dve = sem("slot_ps"), sem("slot_act"), sem("slot_dve")
        give_ps, give_done = sem("give_ps"), sem("give_done")
        g_ps, u_ps, gelu_done, hid_done = sem("g_ps"), sem("u_ps"), sem("gelu_done"), sem("hid_done")
        hidT_ps, hidT_done, down_ps, half_done, eo_done = (
            sem("hidT_ps"), sem("hidT_done"), sem("down_ps"), sem("half_done"), sem("eo_done"))
        eo_sent = [sem(f"eo_sent{i}") for i in range(2)]
        sx_done = sem("sx_done")
        y_ps, y_done, out_sent = sem("y_ps"), sem("y_done"), sem("out_sent")

        PROJ, TRANS, AV, SCORE = (0, 1), (2, 3), 4, (5, 6, 7)
        LN_BANK, RES_BANK = (2, 4, 0), (0, 4)
        LIN_ORDER = [("k", 0), ("k", 1), ("kv", 0), ("k", 2), ("kv", 1), ("k", 3), ("kv", 2),
                     ("q", 0), ("kv", 3), ("q", 1), ("att", 0), ("q", 2), ("q", 3), ("att", 1)]
        QKV_BY = [("act",), ("dve",)] * 2 + [("act", "dve")] * 4 + [("act",), ("dve",)] * 2

        HALF, QUARTER = FF // 2, FF // 4
        SHARED = [("s", 0, 0, HALF), ("s", 0, HALF, HALF)]
        SHARED += [("s", t, q * QUARTER, QUARTER) for t in range(1, NT) for q in range(4)]
        ITEMS, REST = SHARED[:2], SHARED[2:]
        for e in range(E):
            ITEMS.append(("e", e))
            if e in (1, 2, 4, 5, 7, 8, 10, 11, 13, 14):
                ITEMS.append(REST.pop(0))
        ITEMS += REST
        AT = {item: n for n, item in enumerate(ITEMS)}

        def eo_rows(e):
            halves = slice(0, SLOTS), slice(SLOTS, P)
            return halves[e % 2], halves[1 - e % 2]

        def width(n):
            return ITEMS[n][3] if ITEMS[n][0] == "s" else BANK

        def shared_before(n):
            return sum(item[0] == "s" for item in ITEMS[:n])

        def qkv_count(n, who):
            return sum(who in by for by in QKV_BY[:n + 1])

        block = main.enter_context(nc.Block())

        @block.sync
        def _(sp):
            for dt in range(KT):
                sp.dma_start(k_T[:, 0, dt], wk_d[:, dt]).then_inc(wk_in[dt], 16)
                sp.dma_start(ctx_raw[:, dt], ctx_d[0, :, dt]).then_inc(ctx0_in[dt], 16)
            sp.dma_start(k_T[:, 1], wv_d).then_inc(wv_in, 16)
            sp.dma_start(x[:], x_d.rearrange("(t p) d -> p t d", p=P)).then_inc(x_in, 16)
            for tile, src in ((bias_q, bq_d), (bias_k, bk_d), (bias_v, bv_d)):
                sp.dma_start(tile[:], src).then_inc(bias_in, 16)
            sp.dma_start(o_T[:], wq_d).then_inc(wq_in, 16)
            sp.dma_start(bo_rows[:], bo_d.partition_broadcast(P)).then_inc(rows_in, 16)
            with sp.Fori(1, B) as b:
                sp.wait_ge(ctx_split, b + KT - 1)
                sp.dma_start(ctx_raw[:], ctx_d[b]).then_inc(ctx_in, 16)
            sp.dma_start(w_o[:], wo_d).then_inc(wo_in, 16)
            sp.dma_start(w_qkv[:], wqkv_d).then_inc(wqkv_in, 16)
            sp.wait_ge(x_done, NT)
            sp.dma_start(bout_rows[:], bout_d.partition_broadcast(P)).then_inc(rows_in, 16)
            sp.wait_ge(vbd_zero, 2)
            for hh in range(HPT):
                rows = slice(HD * hh, HD * (hh + 1))
                sp.dma_start(proj[rows, :, hh, :], proj_d[:, rows, :].rearrange("t p f -> p t f")).then_inc(proj_in, 16)
            sp.dma_start(w_out[:], wout_d).then_inc(wout_in, 16)
            sp.wait_ge(qkv_ps, 12)
            sp.dma_start(ws_g[:], wsg_d).then_inc(wsg_in, 16)
            sp.dma_start(ws_u[:], wsu_d).then_inc(wsu_in, 16)
            sp.wait_ge(kv_ps, NT * KT)
            sp.dma_start(w_u0[:], wu_d[0]).then_inc(wu_in[0], 16)
            sp.dma_start(w_d0[:], wd_d[0]).then_inc(wd_in[0], 16)
            sp.dma_start(ws_d[:], wsd_d).then_inc(wsd_in, 16)
            sp.wait_ge(x_done, 2 * NT)
            sp.dma_start(gate[:], gate_d).then_inc(gate_in, 16)
            sp.dma_start(w_g0[:], wg_d[0]).then_inc(wg_in[0], 16)
            for e in range(1, E):
                buf = e % 2
                if e >= 2:
                    sp.wait_ge(g_ps, AT["e", e - 2] + 1)
                sp.dma_start(w_g[buf][:], wg_d[e]).then_inc(wg_in[buf], 16)
                if e >= 2:
                    sp.wait_ge(u_ps, AT["e", e - 2] + 1)
                sp.dma_start(w_u[buf][:], wu_d[e]).then_inc(wu_in[buf], 16)
                if e >= 2:
                    sp.wait_ge(down_ps, AT["e", e - 2] + 1)
                sp.dma_start(w_d[buf][:], wd_d[e]).then_inc(wd_in[buf], 16)
            for t in range(NT):
                sp.wait_ge(y_done, t + 1)
                sp.dma_start(out_d[P * t:P * (t + 1), :], x[:, t, :]).then_inc(out_sent, 16)
            sp.wait_ge(out_sent, 16 * NT)

        @block.gpsimd
        def _(pool):
            pool.memset(ident[:], 0.0).then_inc(consts, 1)
            pool.memset(ones[:], 1.0).then_inc(consts, 1)
            pool.memset(q_diag[:], 0.0).then_inc(consts, 1)
            pool.iota(iota_p[:], [[0, 1]], base=0, channel_multiplier=1,
                      allow_small_or_imprecise_dtypes=True).then_inc(consts, 1)
            pool.wait_ge(consts, 4)
            pool.affine_select(out=ident[:], in_=ident[:], compare_op=ALU.not_equal, fill=1.0, base=0,
                               pattern=[[-1, P]], channel_multiplier=1).then_inc(consts, 1)

            def build_diag(b):
                for hh in range(HPT):
                    rows = slice(HD * hh, HD * (hh + 1))
                    cols = slice(L * (hh % 2), L * (hh % 2 + 1))
                    pool.tensor_copy(q_diag[rows, :, hh // 2, cols],
                                     q_T[rows, :, bass.ds(b * L, L)]).then_inc(diag_done, 1)

            def add_row_bias(i, row_bias):
                pool.wait_ge(xn_done, NT * (i + 1))
                for t in range(NT):
                    pool.tensor_tensor(x[:, t, :], x[:, t, :], row_bias[:], ALU.add).then_inc(xbias_done, 1)

            pool.wait_ge(q_done, KT)
            build_diag(0)
            pool.wait_ge(rows_in, 16)
            pool.wait_ge(diag_done, HPT)
            add_row_bias(0, bo_rows)
            pool.wait_ge(xbias_done, NT)
            with pool.Fori(1, B) as b:
                pool.wait_ge(score_ps, b * PAIRS)
                build_diag(b)

            pool.wait_ge(x_done, NT)
            pool.memset(proj[:], 0.0).then_inc(vbd_zero, 1)
            pool.memset(v_bd[:], 0.0).then_inc(vbd_zero, 1)
            pool.wait_ge(vbd_zero, 2)
            for par in range(2):
                rows = slice(L * par, L * (par + 1))
                pool.memset(v_bd[rows, :, :, par, HD:HD + 1], 1.0).then_inc(vbd_zero, 1)
            pool.wait_ge(vbd_zero, 4)
            pool.wait_ge(rows_in, 32)
            add_row_bias(1, bout_rows)
            pool.wait_ge(x_done, 2 * NT)
            pool.memset(spread_i[:], 0.0).then_inc(consts, 1)
            pool.memset(spread_w[:], 0.0).then_inc(consts, 1)
            for e in range(E):
                pool.wait_ge(eo_done, e + 1)
                for b in range(B):
                    pool.dma_start(eo_slot[CAP * e:CAP * (e + 1), b, :],
                                   eo[SLOTS * (e % 2) + CAP * b:SLOTS * (e % 2) + CAP * (b + 1), :]).then_inc(eo_sent[e % 2], 16)

        @block.scalar
        def _(act):
            def ln_std(k):
                for t in range(NT):
                    act.wait_ge(stats_done, NT * k + t + 1)
                    act.activation(std[:, t:t + 1], var_eps[:, t:t + 1], ACT.Sqrt).then_inc(std_done, 1)

            def ln_copy(k):
                for dt in (0, 2):
                    act.wait_ge(xnT_ps, KT * k + dt + 1)
                    act.copy(xn_T[:, dt, :], bank(LN_BANK[k] + dt)).then_inc(xnT_act, 1)

            def ctx_high(b, par):
                act.wait_ge(ctx_in, b * 16)
                act.copy(ctx_hi[:, par], ctx_raw[:]).then_inc(ctx_hi_done, 1)

            def first_high():
                for dt in range(KT):
                    act.wait_ge(wk_in[dt], 16)
                    act.copy(wk_hi[:, dt], k_T[:, 0, dt]).then_inc(w_hi, 1)
                    act.wait_ge(ctx0_in[dt], 16)
                    act.copy(ctx_hi[:, 0, dt], ctx_raw[:, dt]).then_inc(ctx_hi_done, 1)

            def v_out(b, par):
                for st in range(NS):
                    act.wait_ge(v_ps, b * NS + st + 1)
                    act.copy(v_s[:, par, st, :], bank(PROJ[st % 2])).then_inc(v_done, 1)

            def probs_T_out(b):
                for ht in range(KT):
                    act.wait_ge(pT_ps, b * PAIRS + 2 * ht + 1)
                    act.copy(probs_T[:, ht % 2, 0].rearrange("p s c -> p (s c)"), bank(TRANS[0])).then_inc(pT_done[0], 1)

            def exponents(b):
                for p in range(PAIRS):
                    act.wait_ge(max_done, b * PAIRS + p + 1)
                    act.activation(probs[:, p, :], bank(SCORE[p % 3]), ACT.Exp, bias=neg_max[:, p:p + 1], scale=1.0,
                                   accum_out=row_sum[:, p:p + 1]).then_inc(exp_done, 1)

            first_high()
            act.wait_ge(wv_in, 16)
            act.copy(wv_hi[:], k_T[:, 1]).then_inc(w_hi, 1)
            ln_std(0)
            v_out(0, 0)
            ln_copy(0)
            ctx_high(1, 1)
            exponents(0)

            def step(b, par, more=True):
                if more:
                    ctx_high(b + 1, 1 - par)
                probs_T_out(b - 1)
                v_out(b, par)
                exponents(b)

            with act.Fori(1, B - 1, 2) as b:
                step(b, 1)
                step(b + 1, 0)
            step(B - 1, 1, more=False)
            probs_T_out(B - 1)

            ln_std(1)
            ln_copy(1)
            for n in range(12):
                if "act" not in QKV_BY[n]:
                    continue
                act.wait_ge(qkv_ps, n + 1)
                if n < 4:
                    act.copy(kl_T[:, n, :], bank(n % 4)).then_inc(qkv_act, 1)
                elif n < 8:
                    act.wait_ge(vbd_zero, 4)
                    act.copy(v_bd[0:L, n - 4, :, 0, 0:HD],
                             ps[0:L, n % 4, :].rearrange("p (h c) -> p h c", c=HD)).then_inc(qkv_act, 1)
                else:
                    act.copy(ql_T[:, n - 8, :], bank(n % 4)).then_inc(qkv_act, 1)
            u = w = 0
            for kind, i in LIN_ORDER:
                if kind in "kq":
                    for _ in range(4):
                        act.wait_ge(feat_ps, u + 1)
                        if u >= 4:
                            act.wait_ge(feat_done, u - 3)
                        act.activation(exps[:, u % 4, :], bank(u % 3), ACT.Exp).then_inc(fexp_done, 1)
                        if u % 2 == 0:
                            act.activation(relus[:, u // 2 % 2, :], bank(u % 3), ACT.Relu).then_inc(frelu_done, 1)
                        u += 1
                elif kind == "kv":
                    for t in range(NT):
                        act.wait_ge(kv_ps, w + 1)
                        act.copy(kv[:, t, HPT * i:HPT * (i + 1), :],
                                 ps[:, 3 + w % 2, 0:HPT * 2 * KVW].rearrange("p (h c) -> p h c", h=HPT)).then_inc(kv_done, 1)
                        w += 1
            for dt in (0, 2):
                act.wait_ge(attT_ps, dt + 1)
                act.copy(att_T[:, dt, :], bank(dt)).then_inc(attT_act, 1)

            ln_std(2)
            ln_copy(2)
            act.wait_ge(lsub_done, 1)
            act.activation(logit[:], logit[:], ACT.Exp).then_inc(lexp_done, 1)

            def item_gelu(n):
                act.wait_ge(g_ps, n + 1)
                w = width(n)
                act.activation(hid[:, n % 2, 0:w], ps[:, 2 * (n % 2), 0:w], ACT.Gelu).then_inc(gelu_done, 1)

            def item_out(n):
                act.wait_ge(hidT_ps, n + 1)
                w = width(n)
                act.copy(hid_T[:, n % 2].rearrange("p j c -> p (j c)")[:, 0:w], ps[:, 4 + n % 2, 0:w]).then_inc(hidT_done, 1)
                if ITEMS[n][0] == "e":
                    e = ITEMS[n][1]
                    act.wait_ge(down_ps, n + 1)
                    if e >= 2:
                        act.wait_ge(eo_sent[e % 2], 16 * B * (e // 2))
                    mine, other = eo_rows(e)
                    act.copy(eo[mine, :], ps[other, 6 + n % 2, :]).then_inc(half_done, 1)

            item_gelu(0)
            item_gelu(1)
            item_out(0)
            for g in range(0, 2 * KT, 2):
                act.wait_ge(slot_ps, g + 1)
                act.copy(x_slot[:, g // 2, :, 0:32].rearrange("p e (t s) -> p t e s", t=2),
                         bank(5).rearrange("p (t e s) -> p t e s", t=2, e=E)).then_inc(slot_act, 1)
            for n in range(2, len(ITEMS)):
                item_gelu(n)
                item_out(n - 1)
            item_out(len(ITEMS) - 1)

        @block.vector
        def _(dve):
            links = [0]

            def link(ins):
                links[0] += 1
                ins.then_inc(chain, 1)
                dve.wait_ge(chain, links[0])

            def ln_stats(t):
                link(dve.bn_stats(stats[:, t, :], x[:, t, :]))
                link(dve.bn_aggr(mean_var[:, t, :], stats[:, t, :]))
                dve.tensor_scalar(var_eps[:, t:t + 1], mean_var[:, t, 1:2], EPS, None, ALU.add).then_inc(stats_done, 1)

            def ln_rows(k, t, xn):
                r, v, w = rstd[:, t:t + 1], var_eps[:, t:t + 1], newton[:, t:t + 1]
                dve.wait_ge(std_done, NT * k + t + 1)
                link(dve.reciprocal(r, std[:, t:t + 1]))
                link(dve.scalar_tensor_tensor(out=w, in0=r, scalar=r, in1=v, op0=ALU.mult, op1=ALU.mult))
                link(dve.tensor_scalar(w, w, -0.5, 1.5, ALU.mult, ALU.add))
                link(dve.tensor_tensor(r, r, w, ALU.mult))
                dve.tensor_scalar(xn[:, t, :], x[:, t, :], mean_var[:, t, 0:1], r,
                                  ALU.subtract, ALU.mult).then_inc(xn_done, 1)

            def residual_ln(k, xn):
                for t in range(NT):
                    if k:
                        dve.wait_ge(xbias_done, NT * (k - 1) + t + 1)
                        dve.wait_ge(res_ps, NT * (k - 1) + t + 1)
                        dve.tensor_tensor(x[:, t, :], bank(RES_BANK[k - 1] + t), x[:, t, :], ALU.add).then_inc(x_done, 1)
                        dve.wait_ge(x_done, NT * (k - 1) + t + 1)
                    ln_stats(t)
                    if t:
                        ln_rows(k, t - 1, xn)
                ln_rows(k, NT - 1, xn)

            def ln_copy(k):
                for dt in (1, 3):
                    dve.wait_ge(xnT_ps, KT * k + dt + 1)
                    dve.tensor_copy(xn_T[:, dt, :], bank(LN_BANK[k] + dt)).then_inc(xnT_dve, 1)

            def ctx_low(b, par):
                dve.wait_ge(ctx_hi_done, b + KT)
                dve.tensor_tensor(ctx_lo[:, par], ctx_raw[:], ctx_hi[:, par].bitcast(F32),
                                  ALU.subtract).then_inc(ctx_split, 1)

            def w_low(n, lo, raw, hi):
                dve.wait_ge(w_hi, n)
                dve.tensor_tensor(lo, raw, hi.bitcast(F32), ALU.subtract).then_inc(w_split, 1)

            def first_low():
                for dt in range(KT):
                    w_low(dt + 1, wk_lo[:, dt], k_T[:, 0, dt], wk_hi[:, dt])
                    dve.wait_ge(ctx_hi_done, dt + 1)
                    dve.tensor_tensor(ctx_lo[:, 0, dt], ctx_raw[:, dt], ctx_hi[:, 0, dt].bitcast(F32),
                                      ALU.subtract).then_inc(ctx_split, 1)

            def k_out(b, par):
                for ht in range(KT):
                    dve.wait_ge(k_ps, b * KT + ht + 1)
                    dve.tensor_scalar(k_T[:, par, ht, :], bank(PROJ[ht % 2]), bias_k[:, ht:ht + 1], None,
                                      ALU.add).then_inc(k_done, 1)

            def probs_T_out(b):
                for ht in range(KT):
                    dve.wait_ge(pT_ps, b * PAIRS + 2 * ht + 2)
                    dve.tensor_copy(probs_T[:, ht % 2, 1].rearrange("p s c -> p (s c)"), bank(TRANS[1])).then_inc(pT_done[1], 1)

            def o_out(b):
                dve.wait_ge(o_ps, b * KT + KT)
                for hh in range(HPT):
                    rows = slice(HD * hh, HD * (hh + 1))
                    cols = slice(L * (hh % 2), L * (hh % 2 + 1))
                    dve.tensor_tensor(o_T[rows, :, bass.ds(b * L, L)],
                                      bank(AV).rearrange("p (t c) -> p t c", t=KT)[rows, :, cols],
                                      bias_v[rows, :].unsqueeze(2).to_broadcast([HD, KT, L]), ALU.add).then_inc(o_done, 1)

            def normalise(b, p):
                dve.wait_ge(exp_done, b * PAIRS + p + 1)
                dve.reciprocal(row_inv[:, p:p + 1], row_sum[:, p:p + 1]).then_inc(inv_done, 1)
                dve.wait_ge(inv_done, b * PAIRS + p + 1)
                dve.tensor_scalar(probs[:, p, :], probs[:, p, :], row_inv[:, p:p + 1], None,
                                  ALU.mult).then_inc(prob_done, 1)

            def softmax(b):
                for p in range(PAIRS):
                    dve.wait_ge(score_ps, b * PAIRS + p + 1)
                    dve.tensor_reduce(neg_max[:, p:p + 1], bank(SCORE[p % 3]), AX.X, ALU.max,
                                      negate=True).then_inc(max_done, 1)
                    if p:
                        normalise(b, p - 1)
                normalise(b, PAIRS - 1)

            first_low()
            w_low(KT + 1, wv_lo[:], k_T[:, 1], wv_hi[:])
            dve.wait_ge(bias_in, 48)
            dve.wait_ge(w_split, KT + 1)
            k_out(0, 0)
            dve.wait_ge(x_in, 16)
            residual_ln(0, xn_cross)
            ln_copy(0)
            for ht in range(KT):
                dve.wait_ge(q_ps, ht + 1)
                dve.tensor_scalar(q_T[:, ht, :], bank(2 + ht), bias_q[:, ht:ht + 1], HD ** -0.5,
                                  ALU.add, ALU.mult).then_inc(q_done, 1)
            ctx_low(1, 1)
            softmax(0)

            def step(b, par, more=True):
                k_out(b, par)
                probs_T_out(b - 1)
                o_out(b - 1)
                if more:
                    ctx_low(b + 1, 1 - par)
                softmax(b)

            with dve.Fori(1, B - 1, 2) as b:
                step(b, 1)
                step(b + 1, 0)
            step(B - 1, 1, more=False)
            probs_T_out(B - 1)
            o_out(B - 1)

            residual_ln(1, xn_lin)
            ln_copy(1)
            for n in range(12):
                if "dve" not in QKV_BY[n]:
                    continue
                dve.wait_ge(qkv_ps, n + 1)
                if n < 4:
                    dve.tensor_copy(kl_T[:, n, :], bank(n % 4)).then_inc(qkv_dve, 1)
                elif n < 8:
                    dve.wait_ge(vbd_zero, 4)
                    dve.tensor_copy(v_bd[L:P, n - 4, :, 1, 0:HD],
                                    ps[L:P, n % 4, :].rearrange("p (h c) -> p h c", c=HD)).then_inc(qkv_dve, 1)
                else:
                    dve.tensor_copy(ql_T[:, n - 8, :], bank(n % 4)).then_inc(qkv_dve, 1)
            u = a = 0
            for kind, i in LIN_ORDER:
                if kind in "kq":
                    for r in range(4):
                        dve.wait_ge(fexp_done, u + 1)
                        dst = k_feat[:, i % 2, r, :] if kind == "k" else q_feat[:, 4 * i + r, :]
                        if kind == "k" and i >= 2:
                            dve.wait_ge(kv_ps, NT * (i - 1))
                        if u % 2 == 0:
                            dve.wait_ge(frelu_done, u // 2 + 1)
                            dve.scalar_tensor_tensor(out=dst, in0=exps[:, u % 4, :], scalar=1.0,
                                                     in1=relus[:, u // 2 % 2, :], op0=ALU.min,
                                                     op1=ALU.add).then_inc(feat_done, 1)
                        else:
                            link(dve.tensor_scalar(exps[:, u % 4, :], exps[:, u % 4, :], 1.0, None, ALU.min))
                            dve.scalar_tensor_tensor(out=dst, in0=bank(u % 3), scalar=0.0, in1=exps[:, u % 4, :],
                                                     op0=ALU.max, op1=ALU.add).then_inc(feat_done, 1)
                        u += 1
                elif kind == "att":
                    for t in range(NT):
                        dve.wait_ge(att_ps, a + 1)
                        got = ps[:, 5 + a % 2, 0:8 * (HD + 1)].rearrange("p (h c) -> p h c", h=8)
                        link(dve.tensor_scalar(den[:, a, :], got[:, :, HD], 1e-8, None, ALU.add))
                        link(dve.reciprocal(den_inv[:, a, :], den[:, a, :]))
                        dve.tensor_tensor(att[:, t, 256 * i:256 * (i + 1)].rearrange("p (h c) -> p h c", h=8),
                                          got[:, :, 0:HD], den_inv[:, a, :].unsqueeze(2).to_broadcast([P, 8, HD]),
                                          ALU.mult).then_inc(att_done, 1)
                        a += 1
            for dt in (1, 3):
                dve.wait_ge(attT_ps, dt + 1)
                dve.tensor_copy(att_T[:, dt, :], bank(dt)).then_inc(attT_dve, 1)
            residual_ln(2, xn_moe)
            ln_copy(2)

            def over_experts(v):
                return v[:].unsqueeze(2).to_broadcast([P, NT, E])

            def item_hidden(n):
                dve.wait_ge(gelu_done, n + 1)
                dve.wait_ge(u_ps, n + 1)
                w = width(n)
                dve.tensor_tensor(hid[:, n % 2, 0:w], hid[:, n % 2, 0:w], ps[:, 2 * (n % 2) + 1, 0:w],
                                  ALU.mult).then_inc(hid_done, 1)

            def item_sum(n):
                kind, i = ITEMS[n][:2]
                if kind == "s":
                    if shared_before(n):
                        dve.wait_ge(sx_done, shared_before(n))
                    dve.wait_ge(down_ps, n + 1)
                    dve.tensor_tensor(x[:, i, :], bank(6 + n % 2), x[:, i, :], ALU.add).then_inc(sx_done, 1)
                else:
                    dve.wait_ge(half_done, i + 1)
                    mine, _ = eo_rows(i)
                    dve.tensor_tensor(eo[mine, :], ps[mine, 6 + n % 2, :], eo[mine, :], ALU.add).then_inc(eo_done, 1)

            dve.wait_ge(logit_ps, 1)
            got = ps[:, 6, 0:NT * LGW].rearrange("p (t c) -> p t c", t=NT)[:, :, 0:E]
            link(dve.tensor_reduce(lmax[:], got, AX.X, ALU.max))
            dve.tensor_tensor(logit[:], got, over_experts(lmax), ALU.subtract).then_inc(lsub_done, 1)
            dve.wait_ge(lexp_done, 1)
            link(dve.tensor_reduce(lsum[:], logit[:], AX.X, ALU.add))
            link(dve.reciprocal(linv[:], lsum[:]))
            dve.tensor_tensor(logit[:], logit[:], over_experts(linv), ALU.mult).then_inc(score_done, 1)
            dve.wait_ge(scoreT_ps, 1)
            link(dve.tensor_copy(score_T, ps[0:E, 7, :]))
            for b in range(B):
                ins = dve.max(top_w[:, b, :], score_T[:, L * b:L * (b + 1)])
            link(ins)
            for b in range(B):
                ins = dve.max_index(top_i[:, b, :], top_w[:, b, :], score_T[:, L * b:L * (b + 1)])
            link(ins)
            link(dve.tensor_copy(top_f[:], top_i[:]))
            odd = top_f[:].rearrange("e (t u) c -> e t u c", u=2)[:, :, 1, :]
            link(dve.tensor_scalar(odd, odd, float(L), None, ALU.add))
            dve.wait_ge(consts, 7)
            own = ident[0:E, 0:E].unsqueeze(2).to_broadcast([E, E, SLOTS])
            for src, dst in ((top_f, spread_i), (top_w, spread_w)):
                flat = src[:].rearrange("e b c -> e (b c)").unsqueeze(1).to_broadcast([E, E, SLOTS])
                dve.tensor_tensor(dst[0:E], flat, own, ALU.mult).then_inc(spread_done, 1)
            item_hidden(0)
            pick2 = pick[:].rearrange("p e s -> p (e s)")
            for i in range(2):
                dve.wait_ge(pick_ps, i + 1)
                cols = slice(BANK * i, BANK * (i + 1))
                dve.tensor_scalar(pick2[:, cols], bank(4 + i), iota_p[:, 0:1], None, ALU.is_equal).then_inc(pick_done, 1)
            dve.wait_ge(pick_done, 2)
            for i in range(2):
                dve.wait_ge(pick_ps, i + 3)
                half_e = slice(E // 2 * i, E // 2 * (i + 1))
                dve.tensor_tensor(pick_w[:, :, half_e, :].rearrange("p b e c -> p e b c"),
                                  pick[:, half_e, :].rearrange("p e (b c) -> p e b c", b=B),
                                  bank(6 + i).rearrange("p (e b c) -> p e b c", e=E // 2, b=B), ALU.mult).then_inc(pick_done, 1)
            item_hidden(1)
            item_sum(0)
            for g in range(1, 2 * KT, 2):
                dve.wait_ge(slot_ps, g + 1)
                dve.tensor_copy(x_slot[:, g // 2, :, 32:64].rearrange("p e (t s) -> p t e s", t=2),
                                bank(7).rearrange("p (t e s) -> p t e s", t=2, e=E)).then_inc(slot_dve, 1)
            for i in range(2):
                dve.wait_ge(give_ps, i + 1)
                for par in range(2):
                    src = bank(5 + 2 * i).rearrange("p (b u l) -> p b u l", u=2, l=L).rearrange(
                        "p (t v) u l -> p t v u l", v=2)[:, :, par, par, :]
                    dst = give[:, 4 * i:4 * (i + 1), :].rearrange("p (t v) l -> p t v l", v=2)[:, :, par, :]
                    dve.tensor_copy(dst, src).then_inc(give_done, 1)
            for n in range(2, len(ITEMS)):
                item_hidden(n)
                item_sum(n - 1)
            item_sum(len(ITEMS) - 1)
            dve.wait_ge(sx_done, len(SHARED))
            for t in range(NT):
                dve.wait_ge(y_ps, t + 1)
                dve.tensor_tensor(x[:, t, :], bank(t), x[:, t, :], ALU.add).then_inc(y_done, 1)

        @block.tensor
        def _(pe):
            def ln_transpose(k, xn):
                for t in range(NT):
                    pe.wait_ge(xn_done, NT * k + t + 1)
                    for dt in range(KT):
                        ins = pe.transpose(ps[:, LN_BANK[k] + dt, P * t:P * (t + 1)], xn[:, t, P * dt:P * (dt + 1)],
                                           ident[:])
                        if t == NT - 1:
                            ins.then_inc(xnT_ps, 1)

            def xn_T_ready(k):
                pe.wait_ge(xnT_act, 2 * (k + 1))
                pe.wait_ge(xnT_dve, 2 * (k + 1))

            def product3(dst, lhs, rhs):
                (l_hi, l_lo), (r_hi, r_lo) = lhs, rhs
                for dt in range(KT):
                    for i, (a, c) in enumerate(((l_hi, r_hi), (l_hi, r_lo), (l_lo, r_hi))):
                        ins = pe.matmul(dst, a(dt), c(dt), start=(dt == 0 and i == 0), stop=(dt == KT - 1 and i == 2))
                return ins

            def project_k(b, par, first=False):
                pe.wait_ge(ctx_split, b + KT)
                for ht in range(KT):
                    if ht >= 2:
                        pe.wait_ge(k_done, b * KT + ht - 1)
                    elif not first:
                        pe.wait_ge(v_done, b * NS + ht - 1)
                    cols = slice(P * ht, P * (ht + 1))
                    product3(bank(PROJ[ht % 2]),
                             (lambda dt: wk_hi[:, dt, cols], lambda dt: wk_lo[:, dt, cols]),
                             (lambda dt: ctx_hi[:, par, dt, :], lambda dt: ctx_lo[:, par, dt, :])).then_inc(k_ps, 1)

            def project_v(b, par):
                for st in range(NS):
                    if st >= 2:
                        pe.wait_ge(v_done, b * NS + st - 1)
                    else:
                        pe.wait_ge(k_done, b * KT + st + 3)
                    cols = slice(P * st, P * (st + 1))
                    product3(bank(PROJ[st % 2]),
                             (lambda dt: ctx_hi[:, par, dt, cols], lambda dt: ctx_lo[:, par, dt, cols]),
                             (lambda dt: wv_hi[:, dt, :], lambda dt: wv_lo[:, dt, :])).then_inc(v_ps, 1)

            def scores(b, par, first=False):
                pe.wait_ge(diag_done, b * HPT + HPT)
                for p in range(PAIRS):
                    if p % 2 == 0:
                        pe.wait_ge(k_done, b * KT + p // 2 + 1)
                    if not (first and p < 3):
                        pe.wait_ge(exp_done, b * PAIRS + (p - 2 if p >= 3 else (-1, 0, -2)[p]))
                    pe.matmul(bank(SCORE[p % 3]), q_diag[:, p // 2, p % 2, :], k_T[:, par, p // 2, :],
                              start=True, stop=True).then_inc(score_ps, 1)

            def probs_transpose(b, ht):
                for pr in range(2):
                    pe.wait_ge(prob_done, b * PAIRS + 2 * ht + pr + 1)
                    if ht:
                        pe.wait_ge(pT_done[pr], b * KT + ht)
                    for st in range(NS):
                        ins = pe.transpose(ps[:, TRANS[pr], P * st:P * (st + 1)],
                                           probs[:, 2 * ht + pr, P * st:P * (st + 1)], ident[:])
                    ins.then_inc(pT_ps, 1)

            def attend(b, par, ht):
                for pr in range(2):
                    pe.wait_ge(pT_done[pr], b * KT + ht + 1)
                for st in range(NS):
                    for pr in range(2):
                        cols = slice(2 * HD * (2 * ht + pr), 2 * HD * (2 * ht + pr + 1))
                        ins = pe.matmul(ps[64 * pr:64 * (pr + 1), AV, P * ht:P * (ht + 1)], v_s[:, par, st, cols],
                                        probs_T[:, ht % 2, pr, st, :], start=(st == 0), stop=(st == NS - 1),
                                        skip_group_check=True)
                ins.then_inc(o_ps, 1)

            def attention(b, par):
                pe.wait_ge(v_done, b * NS + NS)
                probs_transpose(b, 0)
                for ht in range(1, KT):
                    probs_transpose(b, ht)
                    attend(b, par, ht - 1)
                attend(b, par, KT - 1)

            pe.wait_ge(consts, 5)
            pe.wait_ge(w_split, KT)
            project_k(0, 0, first=True)
            pe.wait_ge(w_split, KT + 1)
            project_v(0, 0)
            ln_transpose(0, xn_cross)
            xn_T_ready(0)
            pe.wait_ge(wq_in, 16)
            for ht in range(KT):
                for dt in range(KT):
                    ins = pe.matmul(bank(2 + ht), o_T[:, dt, P * ht:P * (ht + 1)], xn_T[:, dt, :],
                                    start=(dt == 0), stop=(dt == KT - 1))
                ins.then_inc(q_ps, 1)
            scores(0, 0, first=True)

            def step(b, par):
                project_k(b, par)
                attention(b - 1, 1 - par)
                project_v(b, par)
                scores(b, par)

            with pe.Fori(1, B - 1, 2) as b:
                step(b, 1)
                step(b + 1, 0)
            step(B - 1, 1)
            attention(B - 1, 1)

            def residual(k, rows_T, w):
                for t in range(NT):
                    for dt in range(KT):
                        ins = pe.matmul(bank(RES_BANK[k] + t), rows_T[:, dt, P * t:P * (t + 1)], w[:, dt, :],
                                        start=(dt == 0), stop=(dt == KT - 1))
                    ins.then_inc(res_ps, 1)

            pe.wait_ge(o_done, B * HPT)
            pe.wait_ge(wo_in, 16)
            residual(0, o_T, w_o)

            ln_transpose(1, xn_lin)
            xn_T_ready(1)
            pe.wait_ge(wqkv_in, 16)

            def qkv_out(n):
                if "act" in QKV_BY[n]:
                    pe.wait_ge(qkv_act, qkv_count(n, "act"))
                if "dve" in QKV_BY[n]:
                    pe.wait_ge(qkv_dve, qkv_count(n, "dve"))

            for n in range(12):
                if n >= 4:
                    qkv_out(n - 4)
                for dt in range(KT):
                    if 4 <= n < 8:
                        t = n - 4
                        a, c = xn_T[:, dt, P * t:P * (t + 1)], w_qkv[:, dt, 2 * D:3 * D]
                    else:
                        at = D + P * n if n < 4 else P * (n - 8)
                        a, c = w_qkv[:, dt, at:at + P], xn_T[:, dt, :]
                    ins = pe.matmul(bank(n % 4), a, c, start=(dt == 0), stop=(dt == KT - 1))
                ins.then_inc(qkv_ps, 1)
            pe.wait_ge(proj_in, 64)
            for n in range(8, 12):
                qkv_out(n)

            u = w = a = 0
            for kind, i in LIN_ORDER:
                if kind in "kq":
                    for r in range(4):
                        if u >= 3:
                            pe.wait_ge(feat_done, u - 2)
                        if kind == "k":
                            lhs, rhs = kl_T[:, i, P * r:P * (r + 1)], proj[:, i].rearrange("p h f -> p (h f)")
                        else:
                            lhs, rhs = proj[:, i, r, :], ql_T[:, i, :]
                        pe.matmul(bank(u % 3), lhs, rhs, start=True, stop=True).then_inc(feat_ps, 1)
                        u += 1
                elif kind == "kv":
                    for t in range(NT):
                        pe.wait_ge(feat_done, (4 * i + t if i < 4 else 0) + 1)
                        if w >= 2:
                            pe.wait_ge(kv_done, w - 1)
                        for hh in range(HPT):
                            ins = pe.matmul(ps[:, 3 + w % 2, 2 * KVW * hh:2 * KVW * (hh + 1)],
                                            k_feat[:, i % 2, t, FEAT * hh:FEAT * (hh + 1)],
                                            v_bd[:, t, HPT * i + hh].rearrange("p u c -> p (u c)"), start=True, stop=True)
                        ins.then_inc(kv_ps, 1)
                        w += 1
                else:
                    pe.wait_ge(kv_done, 8 * (i + 1))
                    pe.wait_ge(feat_done, 16 + 8 * (i + 1))
                    for t in range(NT):
                        if a >= 2:
                            pe.wait_ge(att_done, a - 1)
                        for h in range(8):
                            for par in range(2):
                                b = 2 * t + par
                                ins = pe.matmul(ps[L * par:L * (par + 1), 5 + a % 2, (HD + 1) * h:(HD + 1) * (h + 1)],
                                                q_feat[:, 8 * i + h, L * b:L * (b + 1)],
                                                kv[:, t, 8 * i + h, KVW * par:KVW * par + HD + 1],
                                                start=True, stop=True, skip_group_check=True)
                        ins.then_inc(att_ps, 1)
                        a += 1
            pe.wait_ge(feat_done, 32)
            for t in range(NT):
                pe.wait_ge(att_done, NT + t + 1)
                for dt in range(KT):
                    ins = pe.transpose(ps[:, dt, P * t:P * (t + 1)], att[:, t, P * dt:P * (dt + 1)], ident[:])
                    if t == NT - 1:
                        ins.then_inc(attT_ps, 1)
            pe.wait_ge(attT_act, 2)
            pe.wait_ge(attT_dve, 2)
            pe.wait_ge(wout_in, 16)
            residual(1, att_T, w_out)

            ln_transpose(2, xn_moe)
            xn_T_ready(2)

            def item_up(n, weights, shared, off, in_, shared_in, done):
                dst = 2 * (n % 2) + off
                if ITEMS[n][0] == "e":
                    e = ITEMS[n][1]
                    pe.wait_ge(in_[e % 2], 16 * (e // 2 + 1))
                    for dt in range(KT):
                        for fh in range(2):
                            ins = pe.matmul(ps[64 * fh:64 * (fh + 1), dst, :], x_slot[:, dt, e, :],
                                            weights[e % 2][:, dt, BANK * fh:BANK * (fh + 1)],
                                            start=(dt == 0), stop=(dt == KT - 1), skip_group_check=True)
                else:
                    _, t, f, w = ITEMS[n]
                    pe.wait_ge(shared_in, 16)
                    for dt in range(KT):
                        ins = pe.matmul(ps[:, dst, 0:w], xn_T[:, dt, P * t:P * (t + 1)], shared[:, dt, f:f + w],
                                        start=(dt == 0), stop=(dt == KT - 1))
                ins.then_inc(done, 1)

            def item_gate(n):
                item_up(n, w_g, ws_g, 0, wg_in, wsg_in, g_ps)

            def item_value(n):
                item_up(n, w_u, ws_u, 1, wu_in, wsu_in, u_ps)

            def item_transpose(n):
                pe.wait_ge(hid_done, n + 1)
                for j in range(width(n) // P):
                    ins = pe.transpose(ps[:, 4 + n % 2, P * j:P * (j + 1)], hid[:, n % 2, P * j:P * (j + 1)], ident[:])
                ins.then_inc(hidT_ps, 1)

            def item_down(n):
                pe.wait_ge(hidT_done, n + 1)
                if ITEMS[n][0] == "e":
                    e = ITEMS[n][1]
                    pe.wait_ge(wd_in[e % 2], 16 * (e // 2 + 1))
                    for j in range(KT):
                        for fh in range(2):
                            ins = pe.matmul(ps[64 * fh:64 * (fh + 1), 6 + n % 2, :],
                                            hid_T[:, n % 2, j, 64 * fh:64 * (fh + 1)], w_d[e % 2][:, KT * fh + j, :],
                                            start=(j == 0), stop=(j == KT - 1), skip_group_check=True)
                else:
                    tiles = width(n) // P
                    pe.wait_ge(wsd_in, 16)
                    for j in range(tiles):
                        ins = pe.matmul(bank(6 + n % 2), hid_T[:, n % 2, j, :], ws_d[:, ITEMS[n][2] // P + j, :],
                                        start=(j == 0), stop=(j == tiles - 1))
                ins.then_inc(down_ps, 1)

            pe.wait_ge(gate_in, 16)
            for t in range(NT):
                for dt in range(KT):
                    ins = pe.matmul(ps[:, 6, LGW * t:LGW * (t + 1)], xn_T[:, dt, P * t:P * (t + 1)], gate[:, dt, :],
                                    start=(dt == 0), stop=(dt == KT - 1))
            ins.then_inc(logit_ps, 1)
            item_gate(0)
            pe.wait_ge(score_done, 1)
            for t in range(NT):
                ins = pe.transpose(ps[0:E, 7, P * t:P * (t + 1)], logit[:, t, :], ident[:])
            ins.then_inc(scoreT_ps, 1)
            item_value(0)
            item_gate(1)
            for k, (src, first) in enumerate(((spread_i, 4), (spread_w, 6))):
                pe.wait_ge(spread_done, k + 1)
                for i in range(2):
                    pe.matmul(bank(first + i), ones[:], src[:].rearrange("p e s -> p (e s)")[:, BANK * i:BANK * (i + 1)],
                              start=True, stop=True).then_inc(pick_ps, 1)
            item_value(1)
            pe.wait_ge(pick_done, 4)
            item_transpose(0)
            item_down(0)
            for g in range(2 * KT):
                if g >= 2:
                    pe.wait_ge(slot_dve if g % 2 else slot_act, g // 2)
                for i in range(2):
                    t = 2 * (g % 2) + i
                    ins = pe.matmul(ps[:, 5 + 2 * (g % 2), 256 * i:256 * (i + 1)], xn_moe[:, t, P * (g // 2):P * (g // 2 + 1)],
                                    pick[:, :, 2 * CAP * t:2 * CAP * (t + 1)], start=True, stop=True)
                ins.then_inc(slot_ps, 1)
            pe.wait_ge(slot_act, KT)
            pe.wait_ge(slot_dve, KT)
            for b in range(B):
                ins = pe.transpose(ps[:, 5 + 2 * (b // 4), P * (b % 4):P * (b % 4 + 1)],
                                   pick_w[:, b].rearrange("p e c -> p (e c)"), ident[:])
                if b % 4 == 3:
                    ins.then_inc(give_ps, 1)
            for n in range(2, len(ITEMS)):
                item_gate(n)
                if n == 2:
                    pe.wait_ge(give_done, 4)
                item_transpose(n - 1)
                item_value(n)
                item_down(n - 1)
            item_transpose(len(ITEMS) - 1)
            item_down(len(ITEMS) - 1)
            for par in range(2):
                pe.wait_ge(eo_sent[par], 16 * B * E // 2)
            for b in range(B):
                rows = slice(L * (b % 2), L * (b % 2 + 1))
                ins = pe.matmul(ps[rows, b // 2, :], give[:, b, :], eo_slot[:, b, :], start=True, stop=True,
                                skip_group_check=True)
                if b % 2:
                    ins.then_inc(y_ps, 1)


def rows_first(w, tiles):
    return np.ascontiguousarray(w.reshape(*w.shape[:-2], tiles, P, w.shape[-1]).swapaxes(-3, -2))


def kernel(**inputs):
    import concourse.bacc as bacc
    from concourse.bass_utils import run_bass_kernel_spmd

    a = {k: np.asarray(v) for k, v in inputs.items()}
    gate = np.zeros((D, LGW), np.float32)
    gate[:, :E] = a["L0_ffn_gate_w"].T
    arrays = {
        "x": np.ascontiguousarray(a["x"].reshape(TOK, D)),
        "ctx": rows_first(a["ctx_1024"].swapaxes(1, 2), KT),
        "wq": rows_first(a["L0_xattn_Wq"], KT),
        "bq": np.ascontiguousarray(a["L0_xattn_bq"].reshape(KT, P).T),
        "wk": rows_first(a["L0_xattn_Wk"], KT),
        "bk": np.ascontiguousarray(a["L0_xattn_bk"].reshape(KT, P).T),
        "wv": rows_first(a["L0_xattn_Wv"], KT),
        "bv": np.ascontiguousarray(a["L0_xattn_bv"].reshape(KT, P).T),
        "wo": rows_first(a["L0_xattn_Wo"], KT),
        "bo": a["L0_xattn_bo"],
        "wqkv": rows_first(a["L0_attn_w_qkv"], KT),
        "proj": np.ascontiguousarray(a["L0_attn_proj_matrix"].reshape(KT, HPT * HD, FEAT)),
        "wout": rows_first(a["L0_attn_w_out"], KT),
        "bout": a["L0_attn_b_out"],
        "gate": rows_first(gate, KT),
        "wg": rows_first(a["L0_ffn_Wg"].swapaxes(1, 2), KT),
        "wu": rows_first(a["L0_ffn_Wu"].swapaxes(1, 2), KT),
        "wd": rows_first(a["L0_ffn_Wd"].swapaxes(1, 2), NF),
        "wsg": rows_first(a["L0_ffn_Ws_g"].T, KT),
        "wsu": rows_first(a["L0_ffn_Ws_u"].T, KT),
        "wsd": rows_first(a["L0_ffn_Ws_d"].T, NF),
    }
    nc = bacc.Bacc("TRN2", target_bir_lowering=False, num_devices=1)
    args = [nc.dram_tensor(f"in_{k}", v.shape, mybir.dt.from_np(v.dtype), kind="ExternalInput").ap() for k, v in arrays.items()]
    out = nc.dram_tensor("out", (TOK, D), F32, kind="ExternalOutput").ap()
    perceiver_block(nc, *args, out)
    r = run_bass_kernel_spmd(nc, [{f"in_{k}": v for k, v in arrays.items()}], core_ids=[0])
    return r.results[0]["out"].reshape(B, L, D)
```

```python
from contextlib import ExitStack

import numpy as np

import concourse.bass as bass
from concourse import mybir

F32 = mybir.dt.float32
F32R = mybir.dt.float32r
U32 = mybir.dt.uint32
ALU = mybir.AluOpType
ACT = mybir.ActivationFunctionType
AX = mybir.AxisListType

P = 128
B, L, S, D = 8, 64, 512, 512
H, HD, FEAT = 16, 32, 128
E, CAP, FF = 16, 8, 1024
TOK = B * L
NT = TOK // P
KT = D // P
NS = S // P
NF = FF // P
HPT = P // HD
PAIRS = H // 2
SLOTS = B * CAP
KVW = 48
LGW = 96
EPS = 1e-5
BANK = 512


def perceiver_block(nc, x_d, ctx_d, wq_d, bq_d, wk_d, bk_d, wv_d, bv_d, wo_d, bo_d, wqkv_d, proj_d,
                    wout_d, bout_d, gate_d, wg_d, wu_d, wd_d, wsg_d, wsu_d, wsd_d, out_d):
    main = ExitStack()
    with main:
        def sb(stack, name, shape, dt=F32):
            return stack.enter_context(nc.sbuf_tensor(name, shape, dt))

        def sem(name):
            return main.enter_context(nc.semaphore(name))

        x = sb(main, "x", [P, NT, D])
        first = ExitStack()
        xn_hi = sb(first, "xn_hi", [P, KT, TOK], F32R)
        first.close()
        xn_T = sb(main, "xn_T", [P, KT, TOK])
        ident = sb(main, "ident", [P, P])
        iota_p = sb(main, "iota_p", [P, 1])
        head_mask = sb(main, "head_mask", [P, 2])
        ones = sb(main, "ones", [P, P])
        stats = sb(main, "stats", [P, NT, 6])
        mean_var = sb(main, "mean_var", [P, NT, 2])
        var_eps = sb(main, "var_eps", [P, NT])
        std = sb(main, "std", [P, NT])
        rstd = sb(main, "rstd", [P, NT])
        newton = sb(main, "newton", [P, NT])

        early = ExitStack()
        w_qkv = sb(early, "w_qkv", [P, KT, 3 * D])
        cross = ExitStack()
        w_o = sb(cross, "w_o", [P, KT, D])
        bo_rows = sb(cross, "bo_rows", [P, D])
        q_twice = sb(cross, "q_twice", [P, PAIRS, TOK])
        wk_hi = sb(cross, "wk_hi", [P, KT, D], F32R)
        wk_lo = sb(cross, "wk_lo", [P, KT, D], F32R)
        wv_hi = sb(cross, "wv_hi", [P, KT, D], F32R)
        wv_lo = sb(cross, "wv_lo", [P, KT, D], F32R)
        ctx_raw = sb(cross, "ctx_raw", [P, KT, S])
        ctx_hi = sb(cross, "ctx_hi", [P, 2, KT, S], F32R)
        ctx_lo = sb(cross, "ctx_lo", [P, 2, KT, S], F32R)
        k_halves = sb(cross, "k_halves", [P, KT, 2, S], F32R)
        v_s = sb(cross, "v_s", [P, NS, D])
        first = ExitStack()
        xn_lo_cross = sb(first, "xn_lo_cross", [P, KT, TOK], F32R)
        wq_hi = sb(first, "wq_hi", [P, KT, D], F32R)
        first.close()
        probs = sb(cross, "probs", [P, PAIRS, S])
        probs_T = sb(cross, "probs_T", [P, 2, 2, NS, P])
        q_diag = sb(cross, "q_diag", [P, 2, PAIRS, P], F32R)
        first = ExitStack()
        wq_lo = sb(first, "wq_lo", [P, KT, D], F32R)
        first.close()
        o_T = sb(cross, "o_T", [P, KT, TOK])
        neg_max = sb(cross, "neg_max", [P, PAIRS])
        row_sum = sb(cross, "row_sum", [P, PAIRS])
        row_inv = sb(cross, "row_inv", [P, PAIRS])
        bias_q = sb(cross, "bias_q", [P, KT])
        bias_k = sb(cross, "bias_k", [P, KT])
        bias_v = sb(cross, "bias_v", [P, KT])
        bias_q_scaled = sb(cross, "bias_q_scaled", [P, KT])
        cross.close()
        xn_cross, wk_raw = probs[:, 0:KT], probs[:, KT:2 * KT]
        wq_raw, wv_raw = o_T, v_s
        linear = ExitStack()
        kl_halves = sb(linear, "kl_halves", [P, KT, 2, TOK], F32R)
        k_feat0 = sb(linear, "k_feat0", [P, NT, HPT * FEAT])
        first = ExitStack()
        xn_lo = sb(first, "xn_lo", [P, KT, TOK], F32R)
        first.close()
        k_feat1 = sb(linear, "k_feat1", [P, NT, HPT * FEAT])
        k_feat = (k_feat0, k_feat1)
        v_bd = sb(linear, "v_bd", [P, NT, H, 2, KVW])
        rows = ExitStack()
        att = sb(rows, "att", [P, NT, D])
        att_T = sb(rows, "att_T", [P, KT, TOK])
        rows.close()
        ql_halves = sb(linear, "ql_halves", [P, KT, 2, TOK], F32R)
        bout_rows = sb(linear, "bout_rows", [P, D])
        proj_hi = sb(linear, "proj_hi", [P, PAIRS, 2, FEAT], F32R)
        first = ExitStack()
        xn_lin = sb(first, "xn_lin", [P, NT, D])
        first.close()
        proj_lo = sb(linear, "proj_lo", [P, PAIRS, 2, FEAT], F32R)
        w_out = sb(linear, "w_out", [P, KT, D])
        first = ExitStack()
        proj_twice = sb(first, "proj_twice", [P, PAIRS, FEAT])
        first.close()
        relus = sb(linear, "relus", [P, 3, BANK])
        exps = sb(linear, "exps", [P, 3, BANK])
        den = sb(linear, "den", [P, 8, 8])
        den_inv = sb(linear, "den_inv", [P, 8, 8])
        first = ExitStack()
        wqkv_hi = sb(first, "wqkv_hi", [P, KT, 3 * D], F32R)
        first.close()
        q_feat = sb(linear, "q_feat", [P, H, TOK])
        first = ExitStack()
        wqkv_lo = sb(first, "wqkv_lo", [P, KT, 3 * D], F32R)
        first.close()
        kv = sb(linear, "kv", [P, NT, H, 2 * KVW])
        linear.close()
        early.close()
        proj_parts = (proj_hi, proj_lo)

        def qkv_cols(part):
            if part < 4:
                return slice(0, KT), slice(D + P * part, D + P * (part + 1))
            if part < 8:
                return slice(part - 4, part - 3), slice(2 * D, 3 * D)
            return slice(0, KT), slice(P * (part - 8), P * (part - 7))

        moe = ExitStack()
        ws_g = sb(moe, "ws_g", [P, KT, FF])
        ws_u = sb(moe, "ws_u", [P, KT, FF])
        w_u0 = sb(moe, "w_u0", [P, KT, FF])
        w_d0 = sb(moe, "w_d0", [P, NF, D])
        ws_d = sb(moe, "ws_d", [P, NF, D])
        x_slot = sb(moe, "x_slot", [P, KT, E, SLOTS])
        router = ExitStack()
        gate = sb(router, "gate", [P, KT, LGW])
        router.close()
        eo = sb(moe, "eo", [P, D])
        give = sb(moe, "give", [P, B, L])
        route = ExitStack()
        xn_moe = sb(route, "xn_moe", [P, NT, D])
        pick = sb(route, "pick", [P, E, SLOTS])
        spread_i = sb(route, "spread_i", [P, E, SLOTS])
        route.close()
        eo_slot = sb(moe, "eo_slot", [P, B, D])
        hid = sb(moe, "hid", [P, 2, BANK])
        top = ExitStack()
        top_w = sb(top, "top_w", [E, B, CAP])
        top_i = sb(top, "top_i", [E, B, CAP], U32)
        top_f = sb(top, "top_f", [E, B, CAP])
        top.close()
        give_last = sb(moe, "give_last", [P, NT, P])
        give_last_T = eo[:].rearrange("p (t h s) -> p t h s", t=NT, h=2)
        late = ExitStack()
        spread_w = sb(late, "spread_w", [P, E, SLOTS])
        late.close()
        hid_T = sb(moe, "hid_T", [P, 2, KT, P])
        pick_w = spread_i[:].rearrange("p e s -> p (e s)").rearrange("p (b e c) -> p b e c", b=B, e=E)
        logit = sb(moe, "logit", [P, NT, E])
        lmax = sb(moe, "lmax", [P, NT])
        lsum = sb(moe, "lsum", [P, NT])
        linv = sb(moe, "linv", [P, NT])
        w_g0 = sb(moe, "w_g0", [P, KT, FF])
        w_g1 = sb(moe, "w_g1", [P, KT, FF])
        w_u1 = sb(moe, "w_u1", [P, KT, FF])
        w_d1 = sb(moe, "w_d1", [P, NF, D])
        w_g, w_u, w_d = (w_g0, w_g1), (w_u0, w_u1), (w_d0, w_d1)
        score_T = give[:].rearrange("p b l -> p (b l)")[0:E]
        moe.close()

        ps = main.enter_context(nc.psum_tensor("ps", [P, 8, BANK], F32))

        def bank(n):
            return ps[:, n, :]

        x_in, wq_in, wv_in, bias_in = (sem(f"{n}_in") for n in ("x", "wq", "wv", "bias"))
        wk_in = [sem(f"wk_in{dt}") for dt in range(KT)]
        ctx0_in = [sem(f"ctx0_in{dt}") for dt in range(KT)]
        ctx_in, wqkv_in, wo_in, wout_in, rows_in = (sem(f"{n}_in") for n in ("ctx", "wqkv", "wo", "wout", "rows"))
        proj_in, gate_in = sem("proj_in"), sem("gate_in")
        wg_in, wu_in, wd_in = ([sem(f"{n}_in{i}") for i in range(2)] for n in ("wg", "wu", "wd"))
        wsg_in, wsu_in, wsd_in = sem("wsg_in"), sem("wsu_in"), sem("wsd_in")
        consts = sem("consts")
        chain = sem("dve_chain")
        stats_done, std_done, xn_done = sem("stats_done"), sem("std_done"), sem("xn_done")
        xnT_ps, xnT_act, xnT_dve = sem("xnT_ps"), sem("xnT_act"), sem("xnT_dve")
        w_hi, w_split, wv_split, wq_split = sem("w_hi"), sem("w_split"), sem("wv_split"), sem("wq_split")
        ctx_hi_done, ctx_split = sem("ctx_hi_done"), sem("ctx_split")
        k_ps, k_hi_done, k_done, v_ps, v_done = sem("k_ps"), sem("k_hi_done"), sem("k_done"), sem("v_ps"), sem("v_done")
        q_ps, q_done, bias_scaled = sem("q_ps"), sem("q_done"), sem("bias_scaled")
        diag_hi_done, diag_done = sem("diag_hi_done"), sem("diag_done")
        score_ps, max_done, exp_done, inv_done, prob_done = (
            sem("score_ps"), sem("max_done"), sem("exp_done"), sem("inv_done"), sem("prob_done"))
        pT_ps = sem("pT_ps")
        pT_done = [sem("pT_done_act"), sem("pT_done_dve")]
        o_ps, o_done = sem("o_ps"), sem("o_done")
        xbias_done, res_ps, x_done = sem("xbias_done"), sem("res_ps"), sem("x_done")
        qkv_hi_done, qkv_lo_dve, qkv_lo_pool = sem("qkv_hi_done"), sem("qkv_lo_dve"), sem("qkv_lo_pool")
        xn_hi_done, xn_split = sem("xn_hi_done"), sem("xn_split")
        qkv_ps, high_done, qkv_act, qkv_dve = sem("qkv_ps"), sem("high_done"), sem("qkv_act"), sem("qkv_dve")
        proj_hi_done, proj_split = sem("proj_hi_done"), sem("proj_split")
        vbd_zero = sem("vbd_zero")
        feat_ps, fexp_done, frelu_done, feat_done = (
            sem("feat_ps"), sem("fexp_done"), sem("frelu_done"), sem("feat_done"))
        kv_ps, kv_done, att_ps, att_done = sem("kv_ps"), [sem("kv_done_act"), sem("kv_done_dve")], sem("att_ps"), sem("att_done")
        attT_ps, attT_act, attT_dve = sem("attT_ps"), sem("attT_act"), sem("attT_dve")
        logit_ps, lsub_done, lexp_done, score_done = (
            sem("logit_ps"), sem("lsub_done"), sem("lexp_done"), sem("score_done"))
        scoreT_ps, spread_done, pick_ps, pick_done = (
            sem("scoreT_ps"), sem("spread_done"), sem("pick_ps"), sem("pick_done"))
        slot_ps, slot_done = sem("slot_ps"), sem("slot_done")
        give_ps, give_done, last_T_done = sem("give_ps"), sem("give_done"), sem("last_T_done")
        last_done = [sem("last_done_act"), sem("last_done_dve")]
        g_ps, u_ps, gelu_done, hid_done = sem("g_ps"), sem("u_ps"), sem("gelu_done"), sem("hid_done")
        hidT_ps, hidT_done, down_ps, half_done, eo_done = (
            sem("hidT_ps"), sem("hidT_done"), sem("down_ps"), sem("half_done"), sem("eo_done"))
        eo_sent = [sem(f"eo_sent{i}") for i in range(2)]
        sx_done = sem("sx_done")
        y_ps, y_done, out_sent = sem("y_ps"), sem("y_done"), sem("out_sent")

        PROJ, TRANS, AV, SCORE = (0, 1), (2, 3), 4, (5, 6, 7)
        FIRST_K = 4
        EARLY_V = 2
        LN_BANK, RES_BANK = (2, 4, 0), (0, 4)
        ATT_BANK = (0, 1, 2, 7)
        LIN_ORDER = [("p", 8, 0), ("k", 0, 0), ("k", 0, 1), ("p", 9, 0), ("k", 0, 2), ("k", 0, 3), ("p", 10, 0), ("p", 11, 0)]
        for ahead, behind in ((("k", 1), ("kv", 0)), (("k", 2), ("kv", 1)), (("k", 3), ("kv", 2)),
                              (("q", 0), ("kv", 3))):
            for r in range(4):
                LIN_ORDER += [(*ahead, r), (*behind, r)]
        LIN_ORDER += [("q", 1, r) for r in range(4)]
        for t in range(NT):
            LIN_ORDER += [("q", 2 + t // 2, 2 * t % 4), ("q", 2 + t // 2, 2 * t % 4 + 1), ("att", 0, t)]
        LIN_ORDER += [("att", 1, t) for t in range(NT)]

        def act_relus(u):
            return u % 2 == 0 or u >= NT * KT

        QKV_BY = [("dve",)] * 4 + [("act", "dve")] * 4 + [("dve",)] * 4

        QUARTER = FF // 4
        SHARED = [("s", t, q * QUARTER, QUARTER) for t in range(NT) for q in range(4)]
        ITEMS, REST = SHARED[:2], SHARED[2:]
        for e in range(E):
            ITEMS.append(("e", e))
            for _ in range(2 if e == E - 3 else 1 if 0 < e < E - 3 else 0):
                ITEMS.append(REST.pop(0))
        AT = {item: n for n, item in enumerate(ITEMS)}
        LAST = len(ITEMS) - 1
        Y_BANK = [n for n in range(8) if n not in (2 * (LAST % 2), 2 * (LAST % 2) + 1, 4 + LAST % 2, 6 + LAST % 2)]

        def eo_rows(e):
            halves = slice(0, SLOTS), slice(SLOTS, P)
            return halves[e % 2], halves[1 - e % 2]

        def width(n):
            return ITEMS[n][3] if ITEMS[n][0] == "s" else BANK

        def shared_before(n):
            return sum(item[0] == "s" for item in ITEMS[:n])

        def qkv_bank(n):
            return n % 4 if n < 8 else n - 4

        def qkv_count(n, who):
            return sum(who in by for by in QKV_BY[:n + 1])

        block = main.enter_context(nc.Block())

        @block.sync
        def _(sp):
            for dt in range(KT):
                sp.dma_start(wk_raw[:, dt], wk_d[:, dt]).then_inc(wk_in[dt], 16)
                sp.dma_start(ctx_raw[:, dt], ctx_d[0, :, dt]).then_inc(ctx0_in[dt], 16)
            for tile, src in ((bias_k, bk_d), (bias_q, bq_d), (bias_v, bv_d)):
                sp.dma_start(tile[:], src).then_inc(bias_in, 16)
            sp.dma_start(x[:], x_d.rearrange("(t p) d -> p t d", p=P)).then_inc(x_in, 16)
            sp.dma_start(wv_raw[:], wv_d).then_inc(wv_in, 16)
            sp.dma_start(wq_raw[:], wq_d).then_inc(wq_in, 16)
            sp.dma_start(bo_rows[:], bo_d.partition_broadcast(P)).then_inc(rows_in, 16)
            with sp.Fori(1, B) as b:
                sp.wait_ge(ctx_split, b + KT - 1)
                sp.dma_start(ctx_raw[:], ctx_d[b]).then_inc(ctx_in, 16)
            sp.dma_start(w_o[:], wo_d).then_inc(wo_in, 16)
            sp.dma_start(w_qkv[:], wqkv_d).then_inc(wqkv_in, 16)
            sp.wait_ge(x_done, NT)
            sp.dma_start(bout_rows[:], bout_d.partition_broadcast(P)).then_inc(rows_in, 16)
            for q in range(4):
                sp.dma_start(proj_twice[HD * q:HD * (q + 1)], proj_d[q % 2]).then_inc(proj_in, 16)
            sp.dma_start(w_out[:], wout_d).then_inc(wout_in, 16)
            sp.wait_ge(xbias_done, 2 * NT)
            sp.dma_start(gate[:], gate_d).then_inc(gate_in, 16)
            sp.wait_ge(qkv_lo_dve, KT)
            sp.wait_ge(qkv_lo_pool, 2 * KT)
            sp.dma_start(ws_g[:], wsg_d).then_inc(wsg_in, 16)
            sp.wait_ge(kv_ps, NT * KT)
            sp.dma_start(ws_u[:], wsu_d).then_inc(wsu_in, 16)
            sp.dma_start(w_u0[:], wu_d[0]).then_inc(wu_in[0], 16)
            sp.dma_start(w_d0[:], wd_d[0]).then_inc(wd_in[0], 16)
            sp.dma_start(ws_d[:], wsd_d).then_inc(wsd_in, 16)
            sp.wait_ge(att_done, 2 * NT)
            sp.dma_start(w_g0[:], wg_d[0]).then_inc(wg_in[0], 16)
            def expert_load(kind, e):
                tiles, src, arrived, used = {"g": (w_g, wg_d, wg_in, g_ps), "u": (w_u, wu_d, wu_in, u_ps),
                                             "d": (w_d, wd_d, wd_in, down_ps)}[kind]
                if e >= 2:
                    sp.wait_ge(used, AT["e", e - 2] + 1)
                sp.dma_start(tiles[e % 2][:], src[e]).then_inc(arrived[e % 2], 16)

            for kind in "gud":
                expert_load(kind, 1)
            for e in range(2, E, 2):
                for kind, ahead in (("g", 0), ("u", 0), ("g", 1), ("d", 0), ("u", 1), ("d", 1)):
                    expert_load(kind, e + ahead)
            for t in range(NT):
                sp.wait_ge(y_done, t + 1)
                sp.dma_start(out_d[P * t:P * (t + 1), :], x[:, t, :]).then_inc(out_sent, 16)
            sp.wait_ge(out_sent, 16 * NT)

        @block.gpsimd
        def _(pool):
            pool.memset(ident[:], 0.0).then_inc(consts, 1)
            pool.memset(ones[:], 1.0).then_inc(consts, 1)
            pool.memset(head_mask[:], 0.0).then_inc(consts, 1)
            pool.iota(iota_p[:], [[0, 1]], base=0, channel_multiplier=1,
                      allow_small_or_imprecise_dtypes=True).then_inc(consts, 1)
            pool.wait_ge(consts, 4)
            for hh in range(HPT):
                pool.memset(head_mask[HD * hh:HD * (hh + 1), hh % 2:hh % 2 + 1], 1.0).then_inc(consts, 1)
            pool.wait_ge(consts, 4 + HPT)
            pool.affine_select(out=ident[:], in_=ident[:], compare_op=ALU.not_equal, fill=1.0, base=0,
                               pattern=[[-1, P]], channel_multiplier=1).then_inc(consts, 1)

            def add_row_bias(i, row_bias):
                pool.wait_ge(xn_done, NT * (i + 1))
                for t in range(NT):
                    pool.tensor_tensor(x[:, t, :], x[:, t, :], row_bias[:], ALU.add).then_inc(xbias_done, 1)

            for dt in range(KT):
                pool.wait_ge(w_hi, KT + dt + 1)
                pool.tensor_tensor(wv_lo[:, dt], wv_raw[:, dt], wv_hi[:, dt].bitcast(F32), ALU.subtract).then_inc(wv_split, 1)
            for dt in range(KT):
                pool.wait_ge(w_hi, 2 * KT + dt + 1)
                pool.tensor_tensor(wq_lo[:, dt], wq_raw[:, dt], wq_hi[:, dt].bitcast(F32), ALU.subtract).then_inc(wq_split, 1)
            pool.wait_ge(rows_in, 16)
            add_row_bias(0, bo_rows)
            pool.wait_ge(x_done, NT)
            pool.memset(v_bd[:], 0.0).then_inc(vbd_zero, 1)
            pool.wait_ge(vbd_zero, 1)
            for par in range(2):
                rows = slice(L * par, L * (par + 1))
                pool.memset(v_bd[rows, :, :, par, HD:HD + 1], 1.0).then_inc(vbd_zero, 1)
            pool.wait_ge(vbd_zero, 3)
            for part in range(4, 12):
                tiles, cols = qkv_cols(part)
                pool.wait_ge(qkv_hi_done, part + 1)
                pool.tensor_tensor(wqkv_lo[:, tiles, cols], w_qkv[:, tiles, cols],
                                   wqkv_hi[:, tiles, cols].bitcast(F32), ALU.subtract).then_inc(qkv_lo_pool, 1)
            pool.wait_ge(rows_in, 32)
            add_row_bias(1, bout_rows)
            pool.wait_ge(x_done, 2 * NT)
            pool.memset(spread_i[:], 0.0).then_inc(consts, 1)
            pool.memset(spread_w[:], 0.0).then_inc(consts, 1)
            pool.wait_ge(logit_ps, 1)
            pool.memset(eo[:], 0.0).then_inc(consts, 1)

        @block.scalar
        def _(act):
            def ln_std(k, tiles=range(NT)):
                for t in tiles:
                    act.wait_ge(stats_done, NT * k + t + 1)
                    act.activation(std[:, t:t + 1], var_eps[:, t:t + 1], ACT.Sqrt).then_inc(std_done, 1)

            def ln_copy(k):
                for dt in (0, 2):
                    act.wait_ge(xnT_ps, KT * k + dt + 1)
                    act.copy(xn_T[:, dt, :], bank(LN_BANK[k] + dt)).then_inc(xnT_act, 1)

            def xn_high(k):
                for dt in range(KT):
                    act.wait_ge(xnT_ps, KT * k + dt + 1)
                    act.copy(xn_hi[:, dt, :], bank(LN_BANK[k] + dt)).then_inc(xn_hi_done, 1)

            def ctx_high(b, par):
                act.wait_ge(ctx_in, b * 16)
                act.copy(ctx_hi[:, par], ctx_raw[:]).then_inc(ctx_hi_done, 1)

            def first_high():
                for dt in range(KT):
                    act.wait_ge(wk_in[dt], 16)
                    act.copy(wk_hi[:, dt], wk_raw[:, dt]).then_inc(w_hi, 1)
                    act.wait_ge(ctx0_in[dt], 16)
                    act.copy(ctx_hi[:, 0, dt], ctx_raw[:, dt]).then_inc(ctx_hi_done, 1)

            def v_out(b, st):
                act.wait_ge(v_ps, b * NS + st + 1)
                act.copy(v_s[:, st, :], bank(PROJ[st % 2])).then_inc(v_done, 1)

            def k_high(b, ht, first=False):
                n = FIRST_K + ht if first else PROJ[ht % 2]
                act.wait_ge(k_ps, b * KT + ht + 1)
                for pr in range(2):
                    rows = slice(64 * pr, 64 * (pr + 1))
                    act.activation(k_halves[rows, ht, pr, :], ps[rows, n, :], ACT.Identity,
                                   bias=bias_k[rows, ht:ht + 1], scale=1.0).then_inc(k_hi_done, 1)

            def q_out(ht):
                act.wait_ge(q_ps, ht + 1)
                for pr in range(2):
                    rows = slice(64 * pr, 64 * (pr + 1))
                    for to in range(2):
                        ins = act.activation(q_twice[64 * to:64 * (to + 1), 2 * ht + pr, :], ps[rows, 2 + ht, :], ACT.Identity,
                                             bias=bias_q_scaled[rows, ht:ht + 1], scale=HD ** -0.5)
                ins.then_inc(q_done, 1)

            def diag_high(b):
                for i in range(2):
                    act.activation(q_diag[:, 0, :, L * i:L * (i + 1)], q_twice[:, :, bass.ds(b * L, L)], ACT.Identity,
                                   scale=head_mask[:, i:i + 1]).then_inc(diag_hi_done, 1)

            def probs_T_out(b, tiles=range(KT)):
                for ht in tiles:
                    act.wait_ge(pT_ps, b * PAIRS + 2 * ht + 1)
                    act.copy(probs_T[:, ht % 2, 0].rearrange("p s c -> p (s c)"), bank(TRANS[0])).then_inc(pT_done[0], 1)

            def values_and_exponents(b, early=0):
                for p in range(PAIRS):
                    if p % 2 == 0 and p // 2 + early < NS:
                        v_out(b, p // 2 + early)
                    act.wait_ge(max_done, b * PAIRS + p + 1)
                    act.activation(probs[:, p, :], bank(SCORE[p % 3]), ACT.Exp, bias=neg_max[:, p:p + 1], scale=1.0,
                                   accum_out=row_sum[:, p:p + 1]).then_inc(exp_done, 1)

            first_high()
            act.wait_ge(bias_in, 48)
            ln_std(0, (0, 1))
            act.wait_ge(wv_in, 16)
            for dt in range(KT):
                act.copy(wv_hi[:, dt], wv_raw[:, dt]).then_inc(w_hi, 1)
            k_high(0, 0, first=True)
            k_high(0, 1, first=True)
            ln_std(0, (2, 3))
            act.wait_ge(wq_in, 16)
            act.wait_ge(w_split, KT)
            for dt in range(KT):
                act.copy(wq_hi[:, dt], wq_raw[:, dt]).then_inc(w_hi, 1)
            act.wait_ge(wv_split, KT)
            v_out(0, 0)
            xn_high(0)
            for st in range(1, EARLY_V):
                v_out(0, st)
            k_high(0, 2, first=True)
            k_high(0, 3, first=True)
            ctx_high(1, 1)
            act.wait_ge(bias_scaled, 1)
            q_out(0)
            q_out(2)
            act.wait_ge(q_done, KT)
            act.wait_ge(consts, HPT + 4)
            diag_high(0)
            values_and_exponents(0, EARLY_V)

            def step(b, par, more=True):
                k_high(b, 0)
                k_high(b, 1)
                act.wait_ge(score_ps, b * PAIRS)
                diag_high(b)
                k_high(b, 2)
                probs_T_out(b - 1, (0,))
                k_high(b, 3)
                probs_T_out(b - 1, (1, 2, 3))
                if more:
                    ctx_high(b + 1, 1 - par)
                values_and_exponents(b)

            with act.Fori(1, B - 1, 2) as b:
                step(b, 1)
                step(b + 1, 0)
            step(B - 1, 1, more=False)
            probs_T_out(B - 1)

            def qkv_high(parts):
                for part in parts:
                    tiles, cols = qkv_cols(part)
                    act.copy(wqkv_hi[:, tiles, cols], w_qkv[:, tiles, cols]).then_inc(qkv_hi_done, 1)

            def heads_high(n, halves, ht):
                act.wait_ge(qkv_ps, n + 1)
                for pr in range(2):
                    rows = slice(64 * pr, 64 * (pr + 1))
                    act.copy(halves[rows, ht, pr, :], ps[rows, qkv_bank(n), :]).then_inc(high_done, 1)

            ln_std(1)
            act.wait_ge(x_done, NT)
            act.wait_ge(wqkv_in, 16)
            qkv_high(range(4))
            xn_high(1)
            qkv_high(range(4, 8))
            for n in range(4):
                heads_high(n, kl_halves, n)
                qkv_high((8 + n,))
            act.wait_ge(proj_in, 64)
            for i in range(2):
                act.activation(proj_hi[:, :, i, :], proj_twice[:], ACT.Identity,
                               scale=head_mask[:, i:i + 1]).then_inc(proj_hi_done, 1)
            for n in range(4, 8):
                act.wait_ge(qkv_ps, n + 1)
                act.wait_ge(vbd_zero, 3)
                act.copy(v_bd[0:L, n - 4, :, 0, 0:HD],
                         ps[0:L, n % 4, :].rearrange("p (h c) -> p h c", c=HD)).then_inc(qkv_act, 1)
            u = w = 0
            for kind, i, r in LIN_ORDER:
                if kind in "kq":
                    act.wait_ge(feat_ps, u + 1)
                    act.activation(exps[:, u % 3, :], bank(u % 3), ACT.Exp).then_inc(fexp_done, 1)
                    if act_relus(u):
                        act.activation(relus[:, u % 3, :], bank(u % 3), ACT.Relu).then_inc(frelu_done, 1)
                    u += 1
                elif kind == "kv":
                    if w % 2 == 0:
                        act.wait_ge(kv_ps, w + 1)
                        act.copy(kv[:, r, HPT * i:HPT * (i + 1), :],
                                 ps[:, 3, 0:HPT * 2 * KVW].rearrange("p (h c) -> p h c", h=HPT)).then_inc(kv_done[0], 1)
                    w += 1
                elif kind == "p":
                    heads_high(i, ql_halves, i - 8)
            for dt in (0, 2):
                act.wait_ge(attT_ps, dt + 1)
                act.copy(att_T[:, dt, :], bank(ATT_BANK[dt])).then_inc(attT_act, 1)

            ln_std(2)
            ln_copy(2)
            act.wait_ge(lsub_done, 1)
            act.activation(logit[:], logit[:], ACT.Exp).then_inc(lexp_done, 1)

            def item_gelu(n):
                act.wait_ge(g_ps, n + 1)
                w = width(n)
                act.activation(hid[:, n % 2, 0:w], ps[:, 2 * (n % 2), 0:w], ACT.Gelu).then_inc(gelu_done, 1)

            def send(n):
                if ITEMS[n][0] == "s":
                    return
                e = ITEMS[n][1]
                act.wait_ge(eo_done, e + 1)
                for b in range(B):
                    act.dma_start(eo_slot[CAP * e:CAP * (e + 1), b, :],
                                  eo[SLOTS * (e % 2) + CAP * b:SLOTS * (e % 2) + CAP * (b + 1), :]).then_inc(eo_sent[e % 2], 16)

            def item_out(n):
                act.wait_ge(hidT_ps, n + 1)
                w = width(n)
                act.copy(hid_T[:, n % 2].rearrange("p j c -> p (j c)")[:, 0:w], ps[:, 4 + n % 2, 0:w]).then_inc(hidT_done, 1)
                if 0 < n < LAST:
                    send(n - 1)
                if n == LAST:
                    act.wait_ge(down_ps, n + 1)
                    act.copy(hid[0:64, n % 2, :], ps[0:64, 6 + n % 2, :]).then_inc(last_done[0], 1)
                elif ITEMS[n][0] == "e":
                    e = ITEMS[n][1]
                    act.wait_ge(down_ps, n + 1)
                    if e >= 2:
                        act.wait_ge(eo_sent[e % 2], 16 * B * (e // 2))
                    mine, other = eo_rows(e)
                    act.copy(eo[mine, :], ps[other, 6 + n % 2, :]).then_inc(half_done, 1)

            item_gelu(0)
            item_gelu(1)
            for g in range(2 * KT):
                half = slice(32 * (g % 2), 32 * (g % 2 + 1))
                act.wait_ge(slot_ps, g + 1)
                act.copy(x_slot[:, g // 2, :, half].rearrange("p e (t s) -> p t e s", t=2),
                         bank(5 + 2 * (g % 2)).rearrange("p (t e s) -> p t e s", t=2, e=E)).then_inc(slot_done, 1)
            item_out(0)
            for n in range(2, LAST):
                item_gelu(n)
                item_out(n - 1)
            item_out(LAST - 1)
            send(LAST - 1)
            item_gelu(LAST)
            item_out(LAST)

        @block.vector
        def _(dve):
            links = [0]

            def link(ins):
                links[0] += 1
                ins.then_inc(chain, 1)
                dve.wait_ge(chain, links[0])

            def ln_stats(t):
                link(dve.bn_stats(stats[:, t, :], x[:, t, :]))
                link(dve.bn_aggr(mean_var[:, t, :], stats[:, t, :]))
                dve.tensor_scalar(var_eps[:, t:t + 1], mean_var[:, t, 1:2], EPS, None, ALU.add).then_inc(stats_done, 1)

            def ln_rows(k, t, xn):
                r, v, w = rstd[:, t:t + 1], var_eps[:, t:t + 1], newton[:, t:t + 1]
                dve.wait_ge(std_done, NT * k + t + 1)
                link(dve.reciprocal(r, std[:, t:t + 1]))
                link(dve.scalar_tensor_tensor(out=w, in0=r, scalar=r, in1=v, op0=ALU.mult, op1=ALU.mult))
                link(dve.tensor_scalar(w, w, -0.5, 1.5, ALU.mult, ALU.add))
                link(dve.tensor_tensor(r, r, w, ALU.mult))
                dve.tensor_scalar(xn[:, t, :], x[:, t, :], mean_var[:, t, 0:1], r,
                                  ALU.subtract, ALU.mult).then_inc(xn_done, 1)

            def residual_ln(k, xn):
                for t in range(NT):
                    dve.wait_ge(xbias_done, NT * (k - 1) + t + 1)
                    dve.wait_ge(res_ps, NT * (k - 1) + t + 1)
                    dve.tensor_tensor(x[:, t, :], bank(RES_BANK[k - 1] + t), x[:, t, :], ALU.add).then_inc(x_done, 1)
                    dve.wait_ge(x_done, NT * (k - 1) + t + 1)
                    ln_stats(t)
                    ln_rows(k, t, xn)

            def ln_copy(k):
                for dt in (1, 3):
                    dve.wait_ge(xnT_ps, KT * k + dt + 1)
                    dve.tensor_copy(xn_T[:, dt, :], bank(LN_BANK[k] + dt)).then_inc(xnT_dve, 1)

            def xn_low(k, lo):
                for dt in range(KT):
                    dve.wait_ge(xn_hi_done, KT * k + dt + 1)
                    dve.tensor_tensor(lo[:, dt, :], bank(LN_BANK[k] + dt), xn_hi[:, dt, :].bitcast(F32),
                                      ALU.subtract).then_inc(xn_split, 1)

            def ctx_low(b, par):
                dve.wait_ge(ctx_hi_done, b + KT)
                dve.tensor_tensor(ctx_lo[:, par], ctx_raw[:], ctx_hi[:, par].bitcast(F32),
                                  ALU.subtract).then_inc(ctx_split, 1)

            def w_low(n, lo, raw, hi):
                dve.wait_ge(w_hi, n)
                dve.tensor_tensor(lo, raw, hi.bitcast(F32), ALU.subtract).then_inc(w_split, 1)

            def first_low():
                for dt in range(KT):
                    w_low(dt + 1, wk_lo[:, dt], wk_raw[:, dt], wk_hi[:, dt])
                    dve.wait_ge(ctx_hi_done, dt + 1)
                    dve.tensor_tensor(ctx_lo[:, 0, dt], ctx_raw[:, dt], ctx_hi[:, 0, dt].bitcast(F32),
                                      ALU.subtract).then_inc(ctx_split, 1)

            def k_low(b, ht, first=False):
                n = FIRST_K + ht if first else PROJ[ht % 2]
                for pr in range(2):
                    rows, to = slice(64 * pr, 64 * (pr + 1)), slice(64 * (1 - pr), 64 * (2 - pr))
                    dve.wait_ge(k_hi_done, (b * KT + ht) * 2 + pr + 1)
                    ins = dve.scalar_tensor_tensor(out=k_halves[to, ht, pr, :], in0=ps[rows, n, :],
                                                   scalar=bias_k[rows, ht:ht + 1],
                                                   in1=k_halves[rows, ht, pr, :].bitcast(F32), op0=ALU.add, op1=ALU.subtract)
                ins.then_inc(k_done, 1)

            def q_out(ht):
                dve.wait_ge(q_ps, ht + 1)
                for pr in range(2):
                    rows = slice(64 * pr, 64 * (pr + 1))
                    for to in range(2):
                        ins = dve.tensor_scalar(q_twice[64 * to:64 * (to + 1), 2 * ht + pr, :], ps[rows, 2 + ht, :],
                                                bias_q[rows, ht:ht + 1], HD ** -0.5, ALU.add, ALU.mult)
                ins.then_inc(q_done, 1)

            def diag_low(b):
                for i in range(2):
                    cols = slice(L * i, L * (i + 1))
                    dve.wait_ge(diag_hi_done, 2 * b + i + 1)
                    ins = dve.scalar_tensor_tensor(out=q_diag[:, 1, :, cols], in0=q_twice[:, :, bass.ds(b * L, L)],
                                                   scalar=head_mask[:, i:i + 1], in1=q_diag[:, 0, :, cols].bitcast(F32),
                                                   op0=ALU.mult, op1=ALU.subtract)
                ins.then_inc(diag_done, 1)

            def probs_T_out(b, tiles=range(KT)):
                for ht in tiles:
                    dve.wait_ge(pT_ps, b * PAIRS + 2 * ht + 2)
                    dve.tensor_copy(probs_T[:, ht % 2, 1].rearrange("p s c -> p (s c)"), bank(TRANS[1])).then_inc(pT_done[1], 1)

            def o_out(b):
                dve.wait_ge(o_ps, b * KT + KT)
                for hh in range(HPT):
                    rows = slice(HD * hh, HD * (hh + 1))
                    cols = slice(L * (hh % 2), L * (hh % 2 + 1))
                    dve.tensor_tensor(o_T[rows, :, bass.ds(b * L, L)],
                                      bank(AV).rearrange("p (t c) -> p t c", t=KT)[rows, :, cols],
                                      bias_v[rows, :].unsqueeze(2).to_broadcast([HD, KT, L]), ALU.add).then_inc(o_done, 1)

            def normalise(b, p):
                dve.wait_ge(exp_done, b * PAIRS + p + 1)
                dve.reciprocal(row_inv[:, p:p + 1], row_sum[:, p:p + 1]).then_inc(inv_done, 1)
                dve.wait_ge(inv_done, b * PAIRS + p + 1)
                dve.tensor_scalar(probs[:, p, :], probs[:, p, :], row_inv[:, p:p + 1], None,
                                  ALU.mult).then_inc(prob_done, 1)

            def softmax(b):
                for p in range(PAIRS):
                    dve.wait_ge(score_ps, b * PAIRS + p + 1)
                    dve.tensor_reduce(neg_max[:, p:p + 1], bank(SCORE[p % 3]), AX.X, ALU.max,
                                      negate=True).then_inc(max_done, 1)
                    if p:
                        normalise(b, p - 1)
                normalise(b, PAIRS - 1)

            first_low()
            dve.wait_ge(bias_in, 48)
            dve.tensor_scalar(bias_q_scaled[:], bias_q[:], HD ** -0.5, None, ALU.mult).then_inc(bias_scaled, 1)
            dve.wait_ge(x_in, 16)
            ln_stats(0)
            ln_stats(1)
            ln_rows(0, 0, xn_cross)
            ln_rows(0, 1, xn_cross)
            k_low(0, 0, first=True)
            k_low(0, 1, first=True)
            ln_stats(2)
            ln_stats(3)
            ln_rows(0, 2, xn_cross)
            ln_rows(0, 3, xn_cross)
            xn_low(0, xn_lo_cross)
            k_low(0, 2, first=True)
            k_low(0, 3, first=True)
            ctx_low(1, 1)
            q_out(1)
            q_out(3)
            diag_low(0)
            softmax(0)

            def step(b, par, more=True):
                k_low(b, 0)
                k_low(b, 1)
                diag_low(b)
                k_low(b, 2)
                probs_T_out(b - 1, (0,))
                k_low(b, 3)
                probs_T_out(b - 1, (1, 2, 3))
                o_out(b - 1)
                if more:
                    ctx_low(b + 1, 1 - par)
                softmax(b)

            with dve.Fori(1, B - 1, 2) as b:
                step(b, 1)
                step(b + 1, 0)
            step(B - 1, 1, more=False)
            probs_T_out(B - 1)
            o_out(B - 1)

            residual_ln(1, xn_lin)

            def qkv_low(part):
                tiles, cols = qkv_cols(part)
                dve.wait_ge(qkv_hi_done, part + 1)
                dve.tensor_tensor(wqkv_lo[:, tiles, cols], w_qkv[:, tiles, cols],
                                  wqkv_hi[:, tiles, cols].bitcast(F32), ALU.subtract).then_inc(qkv_lo_dve, 1)

            highs = [0]

            def heads_low(n, halves, ht):
                for pr in range(2):
                    rows, to = slice(64 * pr, 64 * (pr + 1)), slice(64 * (1 - pr), 64 * (2 - pr))
                    highs[0] += 1
                    dve.wait_ge(high_done, highs[0])
                    ins = dve.tensor_tensor(halves[to, ht, pr, :], ps[rows, qkv_bank(n), :],
                                            halves[rows, ht, pr, :].bitcast(F32), ALU.subtract)
                ins.then_inc(qkv_dve, 1)

            qkv_low(0)
            xn_low(1, xn_lo)
            for n in range(4):
                if n < 3:
                    qkv_low(n + 1)
                heads_low(n, kl_halves, n)
            for i in range(2):
                dve.wait_ge(proj_hi_done, i + 1)
                dve.scalar_tensor_tensor(out=proj_lo[:, :, i, :], in0=proj_twice[:], scalar=head_mask[:, i:i + 1],
                                         in1=proj_hi[:, :, i, :].bitcast(F32), op0=ALU.mult,
                                         op1=ALU.subtract).then_inc(proj_split, 1)
            for n in range(4, 8):
                dve.wait_ge(qkv_ps, n + 1)
                dve.wait_ge(vbd_zero, 3)
                dve.tensor_copy(v_bd[L:P, n - 4, :, 1, 0:HD],
                                ps[L:P, n % 4, :].rearrange("p (h c) -> p h c", c=HD)).then_inc(qkv_dve, 1)
            u = w = a = 0
            for kind, i, r in LIN_ORDER:
                if kind in "kq":
                    dve.wait_ge(fexp_done, u + 1)
                    dst = k_feat[i % 2][:, r, :] if kind == "k" else q_feat[:, 4 * i + r, :]
                    if kind == "k" and i >= 2:
                        dve.wait_ge(kv_ps, NT * (i - 1))
                    if act_relus(u):
                        dve.wait_ge(frelu_done, sum(act_relus(v) for v in range(u + 1)))
                        dve.scalar_tensor_tensor(out=dst, in0=exps[:, u % 3, :], scalar=1.0,
                                                 in1=relus[:, u % 3, :], op0=ALU.min,
                                                 op1=ALU.add).then_inc(feat_done, 1)
                    else:
                        link(dve.tensor_scalar(exps[:, u % 3, :], exps[:, u % 3, :], 1.0, None, ALU.min))
                        dve.scalar_tensor_tensor(out=dst, in0=bank(u % 3), scalar=0.0, in1=exps[:, u % 3, :],
                                                 op0=ALU.max, op1=ALU.add).then_inc(feat_done, 1)
                    u += 1
                elif kind == "p":
                    heads_low(i, ql_halves, i - 8)
                elif kind == "kv":
                    if w % 2:
                        dve.wait_ge(kv_ps, w + 1)
                        dve.tensor_copy(kv[:, r, HPT * i:HPT * (i + 1), :],
                                        ps[:, 4, 0:HPT * 2 * KVW].rearrange("p (h c) -> p h c", h=HPT)).then_inc(kv_done[1], 1)
                    w += 1
                else:
                    dve.wait_ge(att_ps, a + 1)
                    first = 3 + 2 * (a % 2)
                    got = [ps[L * par:L * (par + 1), first:first + 2, 0:HPT * 2 * KVW].rearrange(
                        "p k (h u c) -> p k h u c", h=HPT, u=2)[:, :, :, par, :] for par in range(2)]
                    for par in range(2):
                        ins = dve.tensor_scalar(den[L * par:L * (par + 1), a, :].rearrange("p (k h) -> p k h", k=2),
                                                got[par][:, :, :, HD], 1e-8, None, ALU.add)
                    link(ins)
                    link(dve.reciprocal(den_inv[:, a, :], den[:, a, :]))
                    for par in range(2):
                        rows = slice(L * par, L * (par + 1))
                        ins = dve.tensor_tensor(att[rows, r, 256 * i:256 * (i + 1)].rearrange("p (k h c) -> p k h c", k=2, h=HPT),
                                                got[par][:, :, :, 0:HD],
                                                den_inv[rows, a, :].rearrange("p (k h) -> p k h", k=2).unsqueeze(3).to_broadcast(
                                                    [L, 2, HPT, HD]), ALU.mult)
                    ins.then_inc(att_done, 1)
                    a += 1
            for dt in (1, 3):
                dve.wait_ge(attT_ps, dt + 1)
                dve.tensor_copy(att_T[:, dt, :], bank(ATT_BANK[dt])).then_inc(attT_dve, 1)
            residual_ln(2, xn_moe)
            ln_copy(2)

            def over_experts(v):
                return v[:].unsqueeze(2).to_broadcast([P, NT, E])

            def item_hidden(n):
                dve.wait_ge(gelu_done, n + 1)
                dve.wait_ge(u_ps, n + 1)
                w = width(n)
                dve.tensor_tensor(hid[:, n % 2, 0:w], hid[:, n % 2, 0:w], ps[:, 2 * (n % 2) + 1, 0:w],
                                  ALU.mult).then_inc(hid_done, 1)

            def item_sum(n):
                kind, i = ITEMS[n][:2]
                if kind == "s":
                    if shared_before(n):
                        dve.wait_ge(sx_done, shared_before(n))
                    dve.wait_ge(down_ps, n + 1)
                    dve.tensor_tensor(x[:, i, :], bank(6 + n % 2), x[:, i, :], ALU.add).then_inc(sx_done, 1)
                elif n == LAST:
                    dve.wait_ge(down_ps, n + 1)
                    dve.tensor_copy(hid[64:P, n % 2, :], ps[64:P, 6 + n % 2, :]).then_inc(last_done[1], 1)
                else:
                    dve.wait_ge(half_done, i + 1)
                    mine, _ = eo_rows(i)
                    dve.tensor_tensor(eo[mine, :], ps[mine, 6 + n % 2, :], eo[mine, :], ALU.add).then_inc(eo_done, 1)

            dve.wait_ge(logit_ps, 1)
            got = ps[:, 6, 0:NT * LGW].rearrange("p (t c) -> p t c", t=NT)[:, :, 0:E]
            link(dve.tensor_reduce(lmax[:], got, AX.X, ALU.max))
            dve.tensor_tensor(logit[:], got, over_experts(lmax), ALU.subtract).then_inc(lsub_done, 1)
            dve.wait_ge(lexp_done, 1)
            link(dve.tensor_reduce(lsum[:], logit[:], AX.X, ALU.add))
            link(dve.reciprocal(linv[:], lsum[:]))
            dve.tensor_tensor(logit[:], logit[:], over_experts(linv), ALU.mult).then_inc(score_done, 1)
            dve.wait_ge(scoreT_ps, 1)
            link(dve.tensor_copy(score_T, ps[0:E, 7, :]))
            for b in range(B):
                ins = dve.max(top_w[:, b, :], score_T[:, L * b:L * (b + 1)])
            link(ins)
            for b in range(B):
                ins = dve.max_index(top_i[:, b, :], top_w[:, b, :], score_T[:, L * b:L * (b + 1)])
            link(ins)
            link(dve.tensor_copy(top_f[:], top_i[:]))
            odd = top_f[:].rearrange("e (t u) c -> e t u c", u=2)[:, :, 1, :]
            link(dve.tensor_scalar(odd, odd, float(L), None, ALU.add))
            dve.wait_ge(consts, HPT + 7)
            own = ident[0:E, 0:E].unsqueeze(2).to_broadcast([E, E, SLOTS])

            def spread(src, dst):
                flat = src[:].rearrange("e b c -> e (b c)").unsqueeze(1).to_broadcast([E, E, SLOTS])
                dve.tensor_tensor(dst[0:E], flat, own, ALU.mult).then_inc(spread_done, 1)

            spread(top_f, spread_i)
            pick2 = pick[:].rearrange("p e s -> p (e s)")
            for i in range(2):
                dve.wait_ge(pick_ps, i + 1)
                cols = slice(BANK * i, BANK * (i + 1))
                dve.tensor_scalar(pick2[:, cols], bank(4 + i), iota_p[:, 0:1], None, ALU.is_equal).then_inc(pick_done, 1)
            spread(top_w, spread_w)
            item_hidden(0)
            item_hidden(1)
            dve.wait_ge(pick_done, 2)
            for i in range(2):
                dve.wait_ge(pick_ps, i + 3)
                half_e = slice(E // 2 * i, E // 2 * (i + 1))
                dve.tensor_tensor(pick_w[:, :, half_e, :].rearrange("p b e c -> p e b c"),
                                  pick[:, half_e, :].rearrange("p e (b c) -> p e b c", b=B),
                                  bank(6 - 2 * i).rearrange("p (e b c) -> p e b c", e=E // 2, b=B), ALU.mult).then_inc(pick_done, 1)
            dve.wait_ge(pick_done, 4)
            dve.wait_ge(consts, HPT + 8)
            for t in range(NT):
                slots = slice(2 * CAP * t, 2 * CAP * (t + 1))
                src = pick_w[:, 2 * t:2 * t + 2, E - 1, :].unsqueeze(1).to_broadcast([P, 2, 2, CAP])
                dve.tensor_copy(give_last_T[:, t, :, slots].rearrange("p h (b c) -> p h b c", c=CAP), src).then_inc(last_T_done, 1)
            item_sum(0)
            for i in range(2):
                dve.wait_ge(give_ps, i + 1)
                for par in range(2):
                    src = bank(5 + 2 * i).rearrange("p (b u l) -> p b u l", u=2, l=L).rearrange(
                        "p (t v) u l -> p t v u l", v=2)[:, :, par, par, :]
                    dst = give[:, 4 * i:4 * (i + 1), :].rearrange("p (t v) l -> p t v l", v=2)[:, :, par, :]
                    dve.tensor_copy(dst, src).then_inc(give_done, 1)
            dve.wait_ge(give_ps, 3)
            dve.tensor_copy(give_last[:].rearrange("p t c -> p (t c)"), bank(4)).then_inc(give_done, 1)
            for n in range(2, LAST):
                item_hidden(n)
                item_sum(n - 1)
            item_sum(LAST - 1)
            item_hidden(LAST)
            item_sum(LAST)
            dve.wait_ge(sx_done, len(SHARED))
            for t in range(NT):
                dve.wait_ge(y_ps, t + 1)
                dve.tensor_tensor(x[:, t, :], bank(Y_BANK[t]), x[:, t, :], ALU.add).then_inc(y_done, 1)

        @block.tensor
        def _(pe):
            def ln_transpose(k, xn):
                for t in range(NT):
                    pe.wait_ge(xn_done, NT * k + t + 1)
                    for dt in range(KT):
                        ins = pe.transpose(ps[:, LN_BANK[k] + dt, P * t:P * (t + 1)], xn[:, t, P * dt:P * (dt + 1)],
                                           ident[:])
                        if t == NT - 1:
                            ins.then_inc(xnT_ps, 1)

            def product3(dst, lhs, rhs):
                (l_hi, l_lo), (r_hi, r_lo) = lhs, rhs
                for dt in range(KT):
                    for i, (a, c) in enumerate(((l_hi, r_hi), (l_hi, r_lo), (l_lo, r_hi))):
                        ins = pe.matmul(dst, a(dt), c(dt), start=(dt == 0 and i == 0), stop=(dt == KT - 1 and i == 2))
                return ins

            def first_keys():
                for dt in range(KT):
                    pe.wait_ge(w_split, dt + 1)
                    pe.wait_ge(ctx_split, dt + 1)
                    for ht in range(KT):
                        cols = slice(P * ht, P * (ht + 1))
                        for i, (w, c) in enumerate(((wk_hi, ctx_hi), (wk_hi, ctx_lo), (wk_lo, ctx_hi))):
                            ins = pe.matmul(bank(FIRST_K + ht), w[:, dt, cols], c[:, 0, dt, :],
                                            start=(dt == 0 and i == 0), stop=(dt == KT - 1 and i == 2))
                        if dt == KT - 1:
                            ins.then_inc(k_ps, 1)

            def project_k(b, par, tiles=range(KT)):
                pe.wait_ge(ctx_split, b + KT)
                for ht in tiles:
                    if ht >= 2:
                        pe.wait_ge(k_done, b * KT + ht - 1)
                    else:
                        pe.wait_ge(v_done, b * NS + ht - 1)
                    cols = slice(P * ht, P * (ht + 1))
                    product3(bank(PROJ[ht % 2]),
                             (lambda dt: wk_hi[:, dt, cols], lambda dt: wk_lo[:, dt, cols]),
                             (lambda dt: ctx_hi[:, par, dt, :], lambda dt: ctx_lo[:, par, dt, :])).then_inc(k_ps, 1)

            def project_v(b, par, st, first=False):
                if st >= 2:
                    pe.wait_ge(v_done, b * NS + st - 1)
                elif first:
                    pe.wait_ge(wv_split, KT)
                else:
                    pe.wait_ge(k_done, b * KT + st + 3)
                cols = slice(P * st, P * (st + 1))
                product3(bank(PROJ[st % 2]),
                         (lambda dt: ctx_hi[:, par, dt, cols], lambda dt: ctx_lo[:, par, dt, cols]),
                         (lambda dt: wv_hi[:, dt, :], lambda dt: wv_lo[:, dt, :])).then_inc(v_ps, 1)

            def values_and_scores(b, par, first=False):
                for p in range(PAIRS):
                    early = EARLY_V if first else 0
                    if p % 2 == 0 and p // 2 + early < NS:
                        project_v(b, par, p // 2 + early, first)
                    if p % 2 == 0:
                        pe.wait_ge(k_done, b * KT + (KT if first else p // 2 + 1))
                    if p == 0:
                        pe.wait_ge(diag_done, b + 1)
                    if not (first and p < 3):
                        pe.wait_ge(exp_done, b * PAIRS + (p - 2 if p >= 3 else (-1, 0, -2)[p]))
                    for half in range(2):
                        ins = pe.matmul(bank(SCORE[p % 3]), q_diag[:, half, p, :], k_halves[:, p // 2, p % 2, :],
                                        start=(half == 0), stop=(half == 1))
                    ins.then_inc(score_ps, 1)

            def probs_transpose(b, ht):
                for pr in range(2):
                    pe.wait_ge(prob_done, b * PAIRS + 2 * ht + pr + 1)
                    if ht:
                        pe.wait_ge(pT_done[pr], b * KT + ht)
                    for st in range(NS):
                        ins = pe.transpose(ps[:, TRANS[pr], P * st:P * (st + 1)],
                                           probs[:, 2 * ht + pr, P * st:P * (st + 1)], ident[:])
                    ins.then_inc(pT_ps, 1)

            def attend(b, ht):
                for pr in range(2):
                    pe.wait_ge(pT_done[pr], b * KT + ht + 1)
                for st in range(NS):
                    for pr in range(2):
                        cols = slice(2 * HD * (2 * ht + pr), 2 * HD * (2 * ht + pr + 1))
                        ins = pe.matmul(ps[64 * pr:64 * (pr + 1), AV, P * ht:P * (ht + 1)], v_s[:, st, cols],
                                        probs_T[:, ht % 2, pr, st, :], start=(st == 0), stop=(st == NS - 1),
                                        skip_group_check=True)
                ins.then_inc(o_ps, 1)

            def attention(b):
                pe.wait_ge(v_done, b * NS + NS)
                for ht in range(1, KT):
                    probs_transpose(b, ht)
                    attend(b, ht - 1)
                attend(b, KT - 1)

            pe.wait_ge(consts, HPT + 5)
            first_keys()
            project_v(0, 0, 0, first=True)
            pe.wait_ge(k_done, 2)
            ln_transpose(0, xn_cross)
            for st in range(1, EARLY_V):
                project_v(0, 0, st, first=True)
            pe.wait_ge(wq_split, KT)
            pe.wait_ge(xn_split, KT)
            for ht in range(KT):
                cols = slice(P * ht, P * (ht + 1))
                for dt in range(KT):
                    for i, (w, c) in enumerate(((wq_hi, xn_hi), (wq_hi, xn_lo_cross), (wq_lo, xn_hi))):
                        ins = pe.matmul(bank(2 + ht), w[:, dt, cols], c[:, dt, :],
                                        start=(dt == 0 and i == 0), stop=(dt == KT - 1 and i == 2))
                ins.then_inc(q_ps, 1)
            values_and_scores(0, 0, first=True)

            def step(b, par):
                project_k(b, par, range(KT - 1))
                probs_transpose(b - 1, 0)
                project_k(b, par, (KT - 1,))
                attention(b - 1)
                values_and_scores(b, par)

            with pe.Fori(1, B - 1, 2) as b:
                step(b, 1)
                step(b + 1, 0)
            step(B - 1, 1)
            probs_transpose(B - 1, 0)
            attention(B - 1)

            def residual(k, rows_T, w):
                for t in range(NT):
                    for dt in range(KT):
                        ins = pe.matmul(bank(RES_BANK[k] + t), rows_T[:, dt, P * t:P * (t + 1)], w[:, dt, :],
                                        start=(dt == 0), stop=(dt == KT - 1))
                    ins.then_inc(res_ps, 1)

            pe.wait_ge(o_done, B * HPT)
            pe.wait_ge(wo_in, 16)
            residual(0, o_T, w_o)

            ln_transpose(1, xn_lin)

            def qkv_out(n):
                if "act" in QKV_BY[n]:
                    pe.wait_ge(qkv_act, qkv_count(n, "act"))
                if "dve" in QKV_BY[n]:
                    pe.wait_ge(qkv_dve, qkv_count(n, "dve"))

            def qkv_project(n):
                if 4 <= n < 8:
                    qkv_out(n - 4)
                if n < 4:
                    pe.wait_ge(qkv_lo_dve, n + 1)
                else:
                    pe.wait_ge(qkv_lo_pool, 4 if n < 8 else n - 3)
                w_part = wqkv_hi, wqkv_lo
                xn_part = xn_hi, xn_lo
                for dt in range(KT):
                    if n == 0:
                        pe.wait_ge(xn_split, KT + dt + 1)
                    for i, (wi, xi) in enumerate(((0, 0), (0, 1), (1, 0))):
                        if 4 <= n < 8:
                            a = xn_part[xi][:, dt, P * (n - 4):P * (n - 3)]
                            c = w_part[wi][:, dt, 2 * D:3 * D]
                        else:
                            a, c = w_part[wi][:, dt, qkv_cols(n)[1]], xn_part[xi][:, dt, :]
                        ins = pe.matmul(bank(qkv_bank(n)), a, c, start=(dt == 0 and i == 0), stop=(dt == KT - 1 and i == 2))
                ins.then_inc(qkv_ps, 1)

            for n in range(8):
                qkv_project(n)

            u = w = a = 0
            for kind, i, r in LIN_ORDER:
                if kind == "p":
                    qkv_project(i)
                elif kind in "kq":
                    if u == 0:
                        pe.wait_ge(proj_split, 2)
                    if u < 3 or (kind, r) == ("q", 0):
                        qkv_out(4 + u if u < 3 else 8 + i)
                    if u >= 3:
                        pe.wait_ge(feat_done, u - 2)
                    if kind == "k":
                        for pr in range(2):
                            for part in range(2):
                                ins = pe.matmul(ps[:, u % 3, 2 * FEAT * pr:2 * FEAT * (pr + 1)],
                                                kl_halves[:, i, pr, P * r:P * (r + 1)],
                                                proj_parts[part][:, 2 * i + pr].rearrange("p h f -> p (h f)"),
                                                start=(part == 0), stop=(part == 1))
                    else:
                        for part in range(2):
                            ins = pe.matmul(bank(u % 3), proj_parts[part][:, 2 * i + r // 2, r % 2, :],
                                            ql_halves[:, i, r // 2, :], start=(part == 0), stop=(part == 1))
                    ins.then_inc(feat_ps, 1)
                    u += 1
                elif kind == "kv":
                    pe.wait_ge(feat_done, 4 * i + r + 1)
                    if w >= 2:
                        pe.wait_ge(kv_done[w % 2], w // 2)
                    else:
                        qkv_out(7 + w)
                    for hh in range(HPT):
                        ins = pe.matmul(ps[:, 3 + w % 2, 2 * KVW * hh:2 * KVW * (hh + 1)],
                                        k_feat[i % 2][:, r, FEAT * hh:FEAT * (hh + 1)],
                                        v_bd[:, r, HPT * i + hh].rearrange("p u c -> p (u c)"), start=True, stop=True)
                    ins.then_inc(kv_ps, 1)
                    w += 1
                else:
                    for done in kv_done:
                        pe.wait_ge(done, NT * KT // 2)
                    pe.wait_ge(feat_done, 16 + 8 * (i + 1))
                    if a >= 2:
                        pe.wait_ge(att_done, a - 1)
                    for h in range(2 * HPT):
                        ins = pe.matmul(ps[:, 3 + 2 * (a % 2) + h // HPT, 2 * KVW * (h % HPT):2 * KVW * (h % HPT + 1)],
                                        q_feat[:, 8 * i + h, P * r:P * (r + 1)], kv[:, r, 8 * i + h, :],
                                        start=True, stop=True)
                    ins.then_inc(att_ps, 1)
                    a += 1
            pe.wait_ge(feat_done, 32)
            for t in range(NT):
                pe.wait_ge(att_done, NT + t + 1)
                for dt in range(KT):
                    ins = pe.transpose(ps[:, ATT_BANK[dt], P * t:P * (t + 1)], att[:, t, P * dt:P * (dt + 1)], ident[:])
                    if t == NT - 1:
                        ins.then_inc(attT_ps, 1)
            pe.wait_ge(attT_act, 2)
            pe.wait_ge(attT_dve, 2)
            pe.wait_ge(wout_in, 16)
            residual(1, att_T, w_out)

            ln_transpose(2, xn_moe)
            pe.wait_ge(xnT_act, 2)
            pe.wait_ge(xnT_dve, 2)

            def item_up(n, weights, shared, off, in_, shared_in, done):
                dst = 2 * (n % 2) + off
                if ITEMS[n][0] == "e":
                    e = ITEMS[n][1]
                    pe.wait_ge(in_[e % 2], 16 * (e // 2 + 1))
                    for dt in range(KT):
                        for fh in range(2):
                            ins = pe.matmul(ps[64 * fh:64 * (fh + 1), dst, :], x_slot[:, dt, e, :],
                                            weights[e % 2][:, dt, BANK * fh:BANK * (fh + 1)],
                                            start=(dt == 0), stop=(dt == KT - 1), skip_group_check=True)
                else:
                    _, t, f, w = ITEMS[n]
                    pe.wait_ge(shared_in, 16)
                    for dt in range(KT):
                        ins = pe.matmul(ps[:, dst, 0:w], xn_T[:, dt, P * t:P * (t + 1)], shared[:, dt, f:f + w],
                                        start=(dt == 0), stop=(dt == KT - 1))
                ins.then_inc(done, 1)

            def item_gate(n):
                item_up(n, w_g, ws_g, 0, wg_in, wsg_in, g_ps)

            def item_value(n):
                item_up(n, w_u, ws_u, 1, wu_in, wsu_in, u_ps)

            def item_transpose(n):
                pe.wait_ge(hid_done, n + 1)
                for j in range(width(n) // P):
                    ins = pe.transpose(ps[:, 4 + n % 2, P * j:P * (j + 1)], hid[:, n % 2, P * j:P * (j + 1)], ident[:])
                ins.then_inc(hidT_ps, 1)

            def item_down(n):
                pe.wait_ge(hidT_done, n + 1)
                if ITEMS[n][0] == "e":
                    e = ITEMS[n][1]
                    pe.wait_ge(wd_in[e % 2], 16 * (e // 2 + 1))
                    for j in range(KT):
                        for fh in range(2):
                            ins = pe.matmul(ps[64 * fh:64 * (fh + 1), 6 + n % 2, :],
                                            hid_T[:, n % 2, j, 64 * fh:64 * (fh + 1)], w_d[e % 2][:, KT * fh + j, :],
                                            start=(j == 0), stop=(j == KT - 1), skip_group_check=True)
                else:
                    tiles = width(n) // P
                    pe.wait_ge(wsd_in, 16)
                    for j in range(tiles):
                        ins = pe.matmul(bank(6 + n % 2), hid_T[:, n % 2, j, :], ws_d[:, ITEMS[n][2] // P + j, :],
                                        start=(j == 0), stop=(j == tiles - 1))
                ins.then_inc(down_ps, 1)

            pe.wait_ge(gate_in, 16)
            for t in range(NT):
                for dt in range(KT):
                    ins = pe.matmul(ps[:, 6, LGW * t:LGW * (t + 1)], xn_T[:, dt, P * t:P * (t + 1)], gate[:, dt, :],
                                    start=(dt == 0), stop=(dt == KT - 1))
            ins.then_inc(logit_ps, 1)
            item_gate(0)
            pe.wait_ge(score_done, 1)
            for t in range(NT):
                ins = pe.transpose(ps[0:E, 7, P * t:P * (t + 1)], logit[:, t, :], ident[:])
            ins.then_inc(scoreT_ps, 1)
            item_value(0)
            item_gate(1)

            def to_all_rows(src, banks):
                for i in range(2):
                    pe.matmul(bank(banks[i]), ones[:], src[:].rearrange("p e s -> p (e s)")[:, BANK * i:BANK * (i + 1)],
                              start=True, stop=True).then_inc(pick_ps, 1)

            pe.wait_ge(spread_done, 1)
            to_all_rows(spread_i, (4, 5))
            item_value(1)
            pe.wait_ge(pick_done, 2)
            for g in range(2 * KT):
                if g >= 2:
                    pe.wait_ge(slot_done, g - 1)
                for i in range(2):
                    t = 2 * (g % 2) + i
                    ins = pe.matmul(ps[:, 5 + 2 * (g % 2), 256 * i:256 * (i + 1)], xn_moe[:, t, P * (g // 2):P * (g // 2 + 1)],
                                    pick[:, :, 2 * CAP * t:2 * CAP * (t + 1)], start=True, stop=True)
                ins.then_inc(slot_ps, 1)
            pe.wait_ge(spread_done, 2)
            to_all_rows(spread_w, (6, 4))
            pe.wait_ge(slot_done, 2 * KT)
            item_gate(2)
            pe.wait_ge(pick_done, 4)
            item_transpose(0)
            item_down(0)
            for b in range(B):
                ins = pe.transpose(ps[:, 5 + 2 * (b // 4), P * (b % 4):P * (b % 4 + 1)],
                                   pick_w[:, b].rearrange("p e c -> p (e c)"), ident[:])
                if b % 4 == 3:
                    ins.then_inc(give_ps, 1)
            pe.wait_ge(last_T_done, NT)
            for t in range(NT):
                ins = pe.transpose(ps[:, 4, P * t:P * (t + 1)], give_last_T[:, t].rearrange("p h s -> p (h s)"), ident[:])
            ins.then_inc(give_ps, 1)
            pe.wait_ge(give_done, 5)
            for n in range(2, LAST):
                if n > 2:
                    item_gate(n)
                item_transpose(n - 1)
                item_value(n)
                item_down(n - 1)
            item_transpose(LAST - 1)
            item_down(LAST - 1)
            item_gate(LAST)
            item_value(LAST)
            for par in range(2):
                pe.wait_ge(eo_sent[par], 16 * B * ((E - par) // 2))
            sent = CAP * (E - 1)
            for b in range(B):
                rows = slice(L * (b % 2), L * (b % 2 + 1))
                pe.matmul(ps[rows, Y_BANK[b // 2], :], give[0:sent, b, :], eo_slot[0:sent, b, :], start=True, stop=False,
                          skip_group_check=True)
            item_transpose(LAST)
            item_down(LAST)
            for part in range(2):
                pe.wait_ge(last_done[part], 1)
            for t in range(NT):
                pe.matmul(bank(Y_BANK[t]), give_last[:, t, :], hid[:, LAST % 2, :], start=False, stop=True,
                          skip_group_check=True).then_inc(y_ps, 1)


def rows_first(w, tiles):
    return np.ascontiguousarray(w.reshape(*w.shape[:-2], tiles, P, w.shape[-1]).swapaxes(-3, -2))


def kernel(**inputs):
    import concourse.bacc as bacc
    from concourse.bass_utils import run_bass_kernel_spmd

    a = {k: np.asarray(v) for k, v in inputs.items()}
    gate = np.zeros((D, LGW), np.float32)
    gate[:, :E] = a["L0_ffn_gate_w"].T
    arrays = {
        "x": np.ascontiguousarray(a["x"].reshape(TOK, D)),
        "ctx": rows_first(a["ctx_1024"].swapaxes(1, 2), KT),
        "wq": rows_first(a["L0_xattn_Wq"], KT),
        "bq": np.ascontiguousarray(a["L0_xattn_bq"].reshape(KT, P).T),
        "wk": rows_first(a["L0_xattn_Wk"], KT),
        "bk": np.ascontiguousarray(a["L0_xattn_bk"].reshape(KT, P).T),
        "wv": rows_first(a["L0_xattn_Wv"], KT),
        "bv": np.ascontiguousarray(a["L0_xattn_bv"].reshape(KT, P).T),
        "wo": rows_first(a["L0_xattn_Wo"], KT),
        "bo": a["L0_xattn_bo"],
        "wqkv": rows_first(a["L0_attn_w_qkv"], KT),
        "proj": np.ascontiguousarray(a["L0_attn_proj_matrix"].reshape(PAIRS, 2, HD, FEAT).transpose(1, 2, 0, 3)),
        "wout": rows_first(a["L0_attn_w_out"], KT),
        "bout": a["L0_attn_b_out"],
        "gate": rows_first(gate, KT),
        "wg": rows_first(a["L0_ffn_Wg"].swapaxes(1, 2), KT),
        "wu": rows_first(a["L0_ffn_Wu"].swapaxes(1, 2), KT),
        "wd": rows_first(a["L0_ffn_Wd"].swapaxes(1, 2), NF),
        "wsg": rows_first(a["L0_ffn_Ws_g"].T, KT),
        "wsu": rows_first(a["L0_ffn_Ws_u"].T, KT),
        "wsd": rows_first(a["L0_ffn_Ws_d"].T, NF),
    }
    nc = bacc.Bacc("TRN2", target_bir_lowering=False, num_devices=1)
    args = [nc.dram_tensor(f"in_{k}", v.shape, mybir.dt.from_np(v.dtype), kind="ExternalInput").ap() for k, v in arrays.items()]
    out = nc.dram_tensor("out", (TOK, D), F32, kind="ExternalOutput").ap()
    perceiver_block(nc, *args, out)
    r = run_bass_kernel_spmd(nc, [{f"in_{k}": v for k, v in arrays.items()}], core_ids=[0])
    return r.results[0]["out"].reshape(B, L, D)
```
